# Optimizing a Trainium2 kernel written in Bass

```python
import numpy as np
import jax
import jax.numpy as jnp

def _softmax(x, axis=-1):
    return jax.nn.softmax(x, axis=axis)

def _gelu(x):
    return jax.nn.gelu(x, approximate=True)

def _silu(x):
    return jax.nn.silu(x)

def _sigmoid(x):
    return jax.nn.sigmoid(x)

def _layernorm(x, axis=-1, eps=1e-05):
    m = jnp.mean(x, axis=axis, keepdims=True)
    v = jnp.var(x, axis=axis, keepdims=True)
    return (x - m) / jnp.sqrt(v + eps)

def _scatter_add(tgt, idx, src, axis=0):
    return tgt.at[idx].add(src)

def _segment_sum(src, seg, n):
    return jax.ops.segment_sum(src, seg, n)
kernel_name = 'mk_seq_preln_d1_jaxref_r8_ca377c'

def setup_inputs(seed: int=0):
    np.random.seed(seed)
    _w = jnp.asarray

    def _L0_attn_setup():
        import jax, jax.numpy as jnp
        import numpy as np
        D_MODEL = 128
        N_HEADS = 16
        ORDER = 6
        P2 = 2 * ORDER - 1
        EPS_CLAMP = 1e-06
        EPS_DEN = 1e-07

        def _beta_np():
            j = np.arange(ORDER, dtype=np.float32)
            alpha = (j + 1.0) ** (-1.5)
            tail = np.flip(np.cumsum(np.flip(alpha)))
            beta = np.concatenate([np.zeros(1, np.float32), tail[1:].astype(np.float32), np.zeros(ORDER - 1, np.float32)])
            return beta / beta.sum()

        def _cheb(x):
            T = [jnp.ones_like(x), x]
            for _ in range(2, P2):
                T.append(2.0 * x * T[-1] - T[-2])
            return jnp.stack(T, axis=3)
        key = jax.random.key(seed)
        k1, k2, k3 = jax.random.split(key, 3)
        B, S, D = (2, 128, D_MODEL)
        x = jax.random.normal(k1, (B, S, D), dtype=jnp.float32)
        W_in = jax.random.normal(k2, (3 * D, D), dtype=jnp.float32) * 0.02
        W_out = jax.random.normal(k3, (D, D), dtype=jnp.float32) * 0.02
        return {'x': x, 'W_in': W_in, 'W_out': W_out}
    _L0_attn_in = _L0_attn_setup()

    def _L0_ffn_setup():
        import jax, jax.numpy as jnp
        import numpy as np
        N_HEAD = 16
        NUM_EXPERTS = 8
        TOP_K = 2
        LN_EPS = 1e-05

        def _layernorm(x, g, b):
            mu = jnp.mean(x, axis=-1, keepdims=True)
            var = jnp.mean(jnp.square(x - mu), axis=-1, keepdims=True)
            return (x - mu) * jax.lax.rsqrt(var + LN_EPS) * g + b

        def _attention(h, Wq, bq, Wk, bk, Wv, bv, Wp, bp):
            B, T, D = h.shape
            hd = D // N_HEAD

            def split(z):
                return z.reshape(B, T, N_HEAD, hd).transpose(0, 2, 1, 3)
            q = split(h @ Wq + bq)
            k = split(h @ Wk + bk)
            v = split(h @ Wv + bv)
            att = jnp.einsum('bhqd,bhkd->bhqk', q, k) / jnp.sqrt(jnp.float32(hd))
            causal = jnp.tril(jnp.ones((T, T), bool))
            att = jnp.where(causal, att, -jnp.inf)
            att = jax.nn.softmax(att, axis=-1)
            y = jnp.einsum('bhqk,bhkd->bhqd', att, v)
            y = y.transpose(0, 2, 1, 3).reshape(B, T, D)
            return y @ Wp + bp

        def _token_moe(h, gate_W, gate_b, exp_W1, exp_b1, exp_W2, exp_b2):
            B, T, D = h.shape
            flat = h.reshape(-1, D)
            N = flat.shape[0]
            logits = flat @ gate_W + gate_b
            top_v, top_i = jax.lax.top_k(logits, TOP_K)
            w = jax.nn.softmax(top_v, axis=-1)
            w_full = jnp.zeros((N, NUM_EXPERTS), flat.dtype)
            w_full = w_full.at[jnp.arange(N)[:, None], top_i].add(w)
            out = jnp.zeros_like(flat)
            for e in range(NUM_EXPERTS):
                mid = jax.nn.gelu(flat @ exp_W1[e] + exp_b1[e], approximate=False)
                y_e = mid @ exp_W2[e] + exp_b2[e]
                out = out + w_full[:, e:e + 1] * y_e
            return out.reshape(B, T, D)
        key = jax.random.key(seed)
        B, T, D = (8, 128, 128)
        H = 4 * D
        E = NUM_EXPERTS
        ks = jax.random.split(key, 24)
        s = 0.02
        inp = {'x': jax.random.normal(ks[0], (B, T, D), jnp.float32), 'ln1_g': jnp.ones((D,), jnp.float32), 'ln1_b': jnp.zeros((D,), jnp.float32), 'ln2_g': jnp.ones((D,), jnp.float32), 'ln2_b': jnp.zeros((D,), jnp.float32), 'Wq': jax.random.normal(ks[1], (D, D), jnp.float32) * s, 'bq': jnp.zeros((D,), jnp.float32), 'Wk': jax.random.normal(ks[2], (D, D), jnp.float32) * s, 'bk': jnp.zeros((D,), jnp.float32), 'Wv': jax.random.normal(ks[3], (D, D), jnp.float32) * s, 'bv': jnp.zeros((D,), jnp.float32), 'Wp': jax.random.normal(ks[4], (D, D), jnp.float32) * s, 'bp': jnp.zeros((D,), jnp.float32), 'gate_W': jax.random.normal(ks[5], (D, E), jnp.float32) * s, 'gate_b': jnp.zeros((E,), jnp.float32), 'exp_W1': jax.random.normal(ks[6], (E, D, H), jnp.float32) * s, 'exp_b1': jnp.zeros((E, H), jnp.float32), 'exp_W2': jax.random.normal(ks[7], (E, H, D), jnp.float32) * s, 'exp_b2': jnp.zeros((E, D), jnp.float32)}
        return inp
    _L0_ffn_in = _L0_ffn_setup()
    _d = {'L0_attn_x': _L0_attn_in['x'], 'L0_attn_W_in': _L0_attn_in['W_in'], 'L0_attn_W_out': _L0_attn_in['W_out'], 'L0_ffn_ln1_g': _L0_ffn_in['ln1_g'], 'L0_ffn_ln1_b': _L0_ffn_in['ln1_b'], 'L0_ffn_ln2_g': _L0_ffn_in['ln2_g'], 'L0_ffn_ln2_b': _L0_ffn_in['ln2_b'], 'L0_ffn_Wq': _L0_ffn_in['Wq'], 'L0_ffn_bq': _L0_ffn_in['bq'], 'L0_ffn_Wk': _L0_ffn_in['Wk'], 'L0_ffn_bk': _L0_ffn_in['bk'], 'L0_ffn_Wv': _L0_ffn_in['Wv'], 'L0_ffn_bv': _L0_ffn_in['bv'], 'L0_ffn_Wp': _L0_ffn_in['Wp'], 'L0_ffn_bp': _L0_ffn_in['bp'], 'L0_ffn_gate_W': _L0_ffn_in['gate_W'], 'L0_ffn_gate_b': _L0_ffn_in['gate_b'], 'L0_ffn_exp_W1': _L0_ffn_in['exp_W1'], 'L0_ffn_exp_b1': _L0_ffn_in['exp_b1'], 'L0_ffn_exp_W2': _L0_ffn_in['exp_W2'], 'L0_ffn_exp_b2': _L0_ffn_in['exp_b2']}
    _x0 = _d['L0_attn_x']
    _d['L0_attn_x'] = jax.random.normal(jax.random.fold_in(jax.random.key(seed), 1), (16, 512, 128), dtype=_x0.dtype)
    del _x0
    return _d

def reference(L0_attn_x, L0_attn_W_in, L0_attn_W_out, L0_ffn_ln1_g, L0_ffn_ln1_b, L0_ffn_ln2_g, L0_ffn_ln2_b, L0_ffn_Wq, L0_ffn_bq, L0_ffn_Wk, L0_ffn_bk, L0_ffn_Wv, L0_ffn_bv, L0_ffn_Wp, L0_ffn_bp, L0_ffn_gate_W, L0_ffn_gate_b, L0_ffn_exp_W1, L0_ffn_exp_b1, L0_ffn_exp_W2, L0_ffn_exp_b2):

    def _L0_attn_ref(x, W_in, W_out):
        import jax, jax.numpy as jnp
        import numpy as np
        D_MODEL = 128
        N_HEADS = 16
        ORDER = 6
        P2 = 2 * ORDER - 1
        EPS_CLAMP = 1e-06
        EPS_DEN = 1e-07

        def _beta_np():
            j = np.arange(ORDER, dtype=np.float32)
            alpha = (j + 1.0) ** (-1.5)
            tail = np.flip(np.cumsum(np.flip(alpha)))
            beta = np.concatenate([np.zeros(1, np.float32), tail[1:].astype(np.float32), np.zeros(ORDER - 1, np.float32)])
            return beta / beta.sum()

        def _cheb(x):
            T = [jnp.ones_like(x), x]
            for _ in range(2, P2):
                T.append(2.0 * x * T[-1] - T[-2])
            return jnp.stack(T, axis=3)
        B, S, D = x.shape
        H, Dh = (N_HEADS, D // N_HEADS)
        qkv = jnp.einsum('bsd,ed->bse', x, W_in)
        q, k, v = jnp.split(qkv, 3, axis=-1)
        q = q.reshape(B, S, H, Dh).transpose(0, 2, 1, 3)
        k = k.reshape(B, S, H, Dh).transpose(0, 2, 1, 3)
        v = v.reshape(B, S, H, Dh).transpose(0, 2, 1, 3)
        inv_sqrt_d = 1.0 / jnp.sqrt(jnp.float32(Dh))
        xq = jnp.clip(q * inv_sqrt_d, -1.0 + EPS_CLAMP, 1.0 - EPS_CLAMP)
        xk = jnp.clip(k * inv_sqrt_d, -1.0 + EPS_CLAMP, 1.0 - EPS_CLAMP)
        Tq = _cheb(xq)
        Tk = _cheb(xk)
        beta = jnp.asarray(_beta_np())
        Tv = Tk * v[:, :, :, None, :]
        kv_prefix = jnp.cumsum(Tv, axis=2)
        ks_prefix = jnp.cumsum(Tk.sum(axis=-1), axis=2)
        kv_beta = kv_prefix * beta[None, None, None, :, None]
        k_beta = ks_prefix * beta[None, None, None, :]
        num = (Tq * kv_beta).sum(axis=3)
        den = (Tq.sum(axis=-1) * k_beta).sum(axis=3)
        out_h = num / (den[..., None] + EPS_DEN)
        out = out_h.transpose(0, 2, 1, 3).reshape(B, S, H * Dh)
        return jnp.einsum('bsd,ed->bse', out, W_out)

    def _L0_ffn_ref(x, ln1_g, ln1_b, ln2_g, ln2_b, Wq, bq, Wk, bk, Wv, bv, Wp, bp, gate_W, gate_b, exp_W1, exp_b1, exp_W2, exp_b2):
        import jax, jax.numpy as jnp
        import numpy as np
        N_HEAD = 16
        NUM_EXPERTS = 8
        TOP_K = 2
        LN_EPS = 1e-05

        def _layernorm(x, g, b):
            mu = jnp.mean(x, axis=-1, keepdims=True)
            var = jnp.mean(jnp.square(x - mu), axis=-1, keepdims=True)
            return (x - mu) * jax.lax.rsqrt(var + LN_EPS) * g + b

        def _attention(h, Wq, bq, Wk, bk, Wv, bv, Wp, bp):
            B, T, D = h.shape
            hd = D // N_HEAD

            def split(z):
                return z.reshape(B, T, N_HEAD, hd).transpose(0, 2, 1, 3)
            q = split(h @ Wq + bq)
            k = split(h @ Wk + bk)
            v = split(h @ Wv + bv)
            att = jnp.einsum('bhqd,bhkd->bhqk', q, k) / jnp.sqrt(jnp.float32(hd))
            causal = jnp.tril(jnp.ones((T, T), bool))
            att = jnp.where(causal, att, -jnp.inf)
            att = jax.nn.softmax(att, axis=-1)
            y = jnp.einsum('bhqk,bhkd->bhqd', att, v)
            y = y.transpose(0, 2, 1, 3).reshape(B, T, D)
            return y @ Wp + bp

        def _token_moe(h, gate_W, gate_b, exp_W1, exp_b1, exp_W2, exp_b2):
            B, T, D = h.shape
            flat = h.reshape(-1, D)
            N = flat.shape[0]
            logits = flat @ gate_W + gate_b
            top_v, top_i = jax.lax.top_k(logits, TOP_K)
            w = jax.nn.softmax(top_v, axis=-1)
            w_full = jnp.zeros((N, NUM_EXPERTS), flat.dtype)
            w_full = w_full.at[jnp.arange(N)[:, None], top_i].add(w)
            out = jnp.zeros_like(flat)
            for e in range(NUM_EXPERTS):
                mid = jax.nn.gelu(flat @ exp_W1[e] + exp_b1[e], approximate=False)
                y_e = mid @ exp_W2[e] + exp_b2[e]
                out = out + w_full[:, e:e + 1] * y_e
            return out.reshape(B, T, D)
        x = x + _attention(_layernorm(x, ln1_g, ln1_b), Wq, bq, Wk, bk, Wv, bv, Wp, bp)
        x = x + _token_moe(_layernorm(x, ln2_g, ln2_b), gate_W, gate_b, exp_W1, exp_b1, exp_W2, exp_b2)
        return x
    x = L0_attn_x
    x = x + _L0_attn_ref(_layernorm(x, axis=-1), L0_attn_W_in, L0_attn_W_out)
    x = x + _L0_ffn_ref(_layernorm(x, axis=-1), L0_ffn_ln1_g, L0_ffn_ln1_b, L0_ffn_ln2_g, L0_ffn_ln2_b, L0_ffn_Wq, L0_ffn_bq, L0_ffn_Wk, L0_ffn_bk, L0_ffn_Wv, L0_ffn_bv, L0_ffn_Wp, L0_ffn_bp, L0_ffn_gate_W, L0_ffn_gate_b, L0_ffn_exp_W1, L0_ffn_exp_b1, L0_ffn_exp_W2, L0_ffn_exp_b2)
    return x

_drawn_inputs = setup_inputs


def setup_inputs(seed=0):
    import zlib

    import numpy as np

    out = dict(_drawn_inputs(seed))
    spreads = {'L0_ffn_ln1_g': (1.0, 0.6),
     'L0_ffn_ln1_b': (0.0, 0.8),
     'L0_ffn_ln2_g': (1.0, 0.6),
     'L0_ffn_ln2_b': (0.0, 2.0),
     'L0_ffn_bq': (0.0, 0.8),
     'L0_ffn_bk': (0.0, 2.0),
     'L0_ffn_bv': (0.0, 0.604),
     'L0_ffn_bp': (0.0, 0.8),
     'L0_ffn_gate_b': (0.0, 1.377),
     'L0_ffn_exp_b1': (0.0, 2.0),
     'L0_ffn_exp_b2': (0.0, 0.8)}
    factors = {'L0_attn_W_in': 8.0,
     'L0_attn_W_out': 8.0,
     'L0_ffn_Wq': 8.0,
     'L0_ffn_Wk': 8.0,
     'L0_ffn_Wv': 8.0,
     'L0_ffn_Wp': 4.218,
     'L0_ffn_exp_W1': 14.316,
     'L0_ffn_gate_W': 5.209,
     'L0_ffn_exp_W2': 3.521}
    for name, (base, spread) in spreads.items():
        noise = np.random.default_rng([zlib.crc32(name.encode()), seed]).standard_normal(out[name].shape)
        drawn = base * np.exp(spread * noise) if base else spread * noise
        out[name] = jnp.asarray(drawn.astype(out[name].dtype))
    for name, factor in factors.items():
        out[name] = (out[name] * factor).astype(out[name].dtype)
    return out
```

```python
from contextlib import ExitStack

import numpy as np

import concourse.bass as bass
from concourse import mybir

F32 = mybir.dt.float32
BF16 = mybir.dt.bfloat16
U32 = mybir.dt.uint32
ALU = mybir.AluOpType
ACT = mybir.ActivationFunctionType
AX = mybir.AxisListType

P = 128
D = 128
B, T = 16, 512
QT = T // P
H, DH = 16, 8
E, HID = 8, 512
HC = HID // P
ORDERS = 5
EPS_LN = 1e-5
EPS_DEN = 1e-7
CLIP = float(np.float32(1.0) - np.float32(1e-6))
SCALE = float(np.float32(1.0) / np.sqrt(np.float32(DH)))
GRID = 1.5 * 2.0 ** 19
NEG = -1e30
TERMS8 = [(1, 2), (2, 1), (0, 2), (2, 0), (1, 1), (0, 1), (1, 0), (0, 0)]
TERMS6 = [(0, 2), (2, 0), (1, 1), (0, 1), (1, 0), (0, 0)]
PR = 4
CREDIT = 2
MROW = 96

C_ID, C_WS, C_SUM, C_SEL, C_MA, C_MB, C_IO = 0, 128, 144, 208, 720, 848, 976
C_N = 984
V_G1, V_B1, V_G2, V_B2, V_BQ, V_BK, V_EB = 0, 1, 2, 3, 4, 5, 6
V_N = V_EB + E * HC
R_BV, R_BP, R_GB = 0, 128, 256
R_N = 264


def beta():
    j = np.arange(6, dtype=np.float32)
    alpha = (j + 1.0) ** (-1.5)
    tail = np.flip(np.cumsum(np.flip(alpha)))
    b = np.concatenate([np.zeros(1, np.float32), tail[1:].astype(np.float32), np.zeros(5, np.float32)])
    return (b / b.sum()).astype(np.float32)


COEF = [float(beta()[p]) * 4.0 ** (p - 1) for p in range(1, ORDERS + 1)]


def constants():
    c = np.zeros((P, C_N), np.float32)
    i = np.arange(P)
    c[i, C_ID + i] = 1
    for h in range(H):
        for p in range(1, 5):
            c[32 * (p - 1) + h, C_WS + h] = COEF[p - 1]
        c[16 + h, C_WS + h] = COEF[4]
        c[DH * h:DH * h + DH, C_SUM + h] = 1
        c[DH * h:DH * h + DH, C_SUM + 32 + 16 + h] = 1
        for t in range(QT):
            c[H * t + h, C_SEL + P * t + DH * h:C_SEL + P * t + DH * h + DH] = 1
    c[:, C_MA:C_MA + P] = np.where(i[None, :] > i[:, None], NEG, 0)
    c[:, C_MB:C_MB + P] = np.where(i[:, None] > i[None, :], NEG, 0)
    c[:, C_IO:C_IO + E] = np.arange(E)
    return c


def block_kernel(nc, x, consts, cols, rows, w_in, w_out, wq, wk, wv, wp, gate_w, ew1, ew2, eb2, out):
    with ExitStack() as ctx:
        def sb(name, shape, dt=F32):
            return ctx.enter_context(nc.sbuf_tensor(name, shape, dt))

        def sem(name):
            return ctx.enter_context(nc.semaphore(name))

        xs = sb("xs", [P, B * QT, D])
        wfull = sb("wfull", [P, B * QT, E])
        w1_sb = sb("w1_sb", [P, E, HID])
        w2_sb = sb("w2_sb", [P, E * HC, D])
        cst = sb("cst", [P, C_N])
        col = sb("col", [P, V_N])
        row = sb("row", [P, R_N])
        win = sb("win", [P, 3 * D])
        wins = sb("wins", [P, 3, 3 * D], BF16)
        wo_sb = sb("wo_sb", [P, D])
        wq_sb = sb("wq_sb", [P, D])
        wk_sb = sb("wk_sb", [P, D])
        wv_sb = sb("wv_sb", [P, D])
        wp_sb = sb("wp_sb", [P, D])
        gw_sb = sb("gw_sb", [P, E])
        eb2_sb = sb("eb2_sb", [E, D])
        identb = sb("identb", [P, P], BF16)
        maskA = sb("maskA", [P, P], BF16)
        maskB = sb("maskB", [P, P], BF16)
        bqs = sb("bqs", [P, 1])
        one = sb("one", [P, 1])
        negc = sb("negc", [P, 2])
        mhalf = sb("mhalf", [P, QT])

        hn = sb("hn", [P, QT, D])
        hs = sb("hs", [P, QT, D])
        hp = sb("hp", [P, 3, T], BF16)
        F = sb("F", [P, 10, T])
        kv = sb("kv", [P, ORDERS, T])
        va = sb("va", [P, T])
        ksum = sb("ksum", [P, T])
        outT = sb("outT", [P, T])
        den = sb("den", [P, QT * H])
        rdT = sb("rdT", [QT * H, P])
        lnT = sb("lnT", [P, T])
        qs = sb("qs", [P, 3, T], BF16)
        ks = sb("ks", [P, 3, T], BF16)
        nm = sb("nm", [P, QT * H])
        nms = sb("nms", [QT * H, 3, P], BF16)
        nmr = sb("nmr", [QT * H, P])
        stack = sb("stack", [P, 2, H, T], BF16)
        qst = stack[:, 0, :, :]
        kst = stack[:, 1, :, :]
        vaug = sb("vaug", [P, QT, H, 32])
        hk = sb("hk", [P, QT, D])
        pr = sb("pr", [P, PR, 2, T])
        oT = sb("oT", [P, 2, T])
        yt = sb("yt", [P, QT, D])
        yT = sb("yT", [P, T])
        rec = sb("rec", [P, QT, 4])
        hb = sb("hb", [P, QT, D])
        h2 = sb("h2", [P, T])
        lg = sb("lg", [P, QT, E])
        top = sb("top", [P, QT, 8])
        topi = sb("topi", [P, QT, 8], U32)
        topf = sb("topf", [P, QT, 8])
        gt = sb("gt", [P, 4, QT])
        gd = sb("gd", [P, QT])
        oh = sb("oh", [P, 2, QT, E])
        wf = sb("wf", [P, QT, E])
        wfT = sb("wfT", [E, QT, P])
        h2d = nc.dram_tensor("h2d", (B, P, T), F32, kind="Internal").ap()
        norm = {}
        for c in "fb":
            norm[c] = dict(st=sb("st" + c, [P, QT, 6]), mv=sb("mv" + c, [P, QT, 2]), lnv=sb("lnv" + c, [P, 4, QT]),
                           rstd=sb("rstd" + c, [P, QT]),
                           stats=sem("ln_stats_" + c), var=sem("ln_var_" + c), step=sem("ln_step_" + c),
                           ready=sem("ln_rstd_" + c), out=sem("ln_out_" + c))
        h2c = stack[:, :, :, :].rearrange("p a h n -> p (a h n)").bitcast(F32).rearrange("p (s n) -> p s n", n=T)
        hid = F[:, 0:8, :].rearrange("p (e c) n -> p e c n", e=2)

        qx, kx = [F[:, i, :] for i in range(5)], [F[:, 5 + i, :] for i in range(5)]
        hr = F[:, 9, :]
        qf, kf, rq, rk = (F[:, i, :] for i in range(4))
        y = yt[:, :, :].rearrange("p t (h d) -> p t h d", h=H)
        ident = cst[:, C_ID:C_ID + P]

        X, Y, Z, V = (ctx.enter_context(nc.psum_tensor(n, [P, T], F32)) for n in ("front0", "front1", "back0", "back1"))
        ring = [ctx.enter_context(nc.psum_tensor(f"ring{i}", [P, 2, T], F32)) for i in range(2)]

        names = """w_loaded x_loaded e_loaded w_split const_ready pool_const
            tr0 h_grid h_rest h_mid h_split hq_mm hk_mm hv_mm hk_ev hq_ev hv_ev k_clip q_clip k_sq q_sq
            k_t35 q_t35 k_t24 q_t24 ks_mm qs_mm k_scan d_prod den_mm den_eps den_rec rdT_mm rdT_ev rdB_mm
            kv_ready kv_sum qk_prod n_add outT_ready o1_mm x1_ready tr1 lnT_ready aq_mm ak_mm av_mm
            qf_ready kf_ready p1_ready r1_ready p2_ready p3_ready v_ready stack_dma smax_mm smax_red
            nmT_mm n1_ready nr_ready n2_ready n3_ready max_dma h_kept sc_mm exp_ready pr_used pv_ev ot_tr
            rec_ready y_ready yT_mm yT_ev o2_mm x2a x2_ready xsum tr3 h2_ready h2_kept gate_mm lg_ready
            top_ready topi_ready topf_ready g_step g_exp oh_ready wf_ready wfT_mm wfT_ev b2_mm xb_ready
            wf_kept h2_loaded mid_mm mid_ready y2_mm acc_ready stored""".split()
        W = type("Sems", (), {n: sem(n) for n in names})
        TILES = 3 * H // 2

        def wait_apart(engine, semaphore, value):
            engine.wait_ge(semaphore, value)
            engine.nop(nofuse=True)

        def pipelined(engine, body):
            body(None, 0)
            with engine.Fori(0, B - 1) as b:
                body(b, b + 1)
            body(B - 1, None)

        block = ctx.enter_context(nc.Block())

        @block.sync
        def _(sp):
            loads = [(cst, consts), (col, cols), (row, rows), (win, w_in), (wo_sb, w_out), (wq_sb, wq),
                     (wk_sb, wk), (wv_sb, wv), (wp_sb, wp), (gw_sb, gate_w), (eb2_sb, eb2)]
            xv = x.rearrange("b (t p) d -> b p t d", p=P)

            def load_x(b):
                sp.dma_start(xs[:, bass.ds(b * QT, QT), :],
                             xv[bass.ds(b, 1), :, :, :].rearrange("a p t d -> (a p) t d")).then_inc(W.x_loaded, 16)

            load_x(0)
            for dst, src in loads:
                sp.dma_start(dst[:, :], src).then_inc(W.w_loaded, 16)
            sp.wait_ge(W.x_loaded, 16)
            with sp.Fori(1, B) as b:
                load_x(b)
                wait_apart(sp, W.x_loaded, b * 16 + 16)
            sp.dma_start(w1_sb[:, :, :], ew1.rearrange("e d n -> d e n")).then_inc(W.e_loaded, 16)
            for e in range(E):
                sp.dma_start(w2_sb[:, e * HC:(e + 1) * HC, :], ew2[e].rearrange("(c p) d -> p c d", p=P)).then_inc(W.e_loaded, 16)

            def body(back, front):
                if back is not None:
                    sp.wait_ge(W.h2_ready, back + 1)
                    sp.dma_start(h2d[bass.ds(back, 1), :, :].rearrange("a p n -> (a p) n"), h2[:, :]).then_inc(W.h2_kept, 16)
                if front is not None:
                    sp.wait_ge(W.p2_ready, front * 2 + 2)
                    sp.wait_ge(W.p3_ready, front * 2 + 2)
                    if back is not None:
                        sp.wait_ge(W.sc_mm, back * TILES + TILES)
                    for n, (i, j) in enumerate(TERMS6):
                        sp.dma_start(qst[DH * n:DH * n + DH, :, :], qs[:, i, :]).then_inc(W.stack_dma, 16)
                        sp.dma_start(kst[DH * n:DH * n + DH, :, :], ks[:, j, :]).then_inc(W.stack_dma, 16)
                    sp.wait_ge(W.n2_ready, front + 1)
                    sp.wait_ge(W.n3_ready, front + 1)
                    for i in range(3):
                        for t in range(QT):
                            sp.dma_start(qst[MROW + i:MROW + i + 1, :, t * P:(t + 1) * P],
                                         nms[t * H:(t + 1) * H, i, :]).then_inc(W.max_dma, 16)

            pipelined(sp, body)
            sp.wait_ge(W.h2_kept, 16 * B)
            sp.wait_ge(W.sc_mm, B * TILES)
            ov = out.rearrange("b (t p) d -> b p t d", p=P)
            with sp.Fori(0, B) as b:
                sp.dma_start(h2c[:, bass.ds(b, 1), :].rearrange("p a n -> p (a n)"),
                             h2d[bass.ds(b, 1), :, :].rearrange("a p n -> (a p) n")).then_inc(W.h2_loaded, 16)
                wait_apart(sp, W.h2_loaded, b * 16 + 16)
            with sp.Fori(0, B) as b:
                sp.wait_ge(W.acc_ready, b * (E * QT) + E * QT + CREDIT * QT)
                sp.dma_start(ov[bass.ds(b, 1), :, :, :].rearrange("a p t d -> (a p) t d"), xs[:, bass.ds(b * QT, QT), :]).then_inc(W.stored, 16)
            sp.wait_ge(W.stored, 16 * B)

        def ln_stats(c, n, src):
            k = norm[c]
            for t in range(QT):
                nc.vector.bn_stats(k["st"][:, t, :], src(t)).then_inc(k["stats"], 1)
            wait_apart(nc.vector, k["stats"], n * QT + QT)
            for t in range(QT):
                nc.vector.bn_aggr(k["mv"][:, t, :], k["st"][:, t, :]).then_inc(k["var"], 1)

        def ln_rsqrt(c, n):
            g, k = nc.gpsimd, norm[c]
            ve, y0, a, b_ = (k["lnv"][:, i, :] for i in range(4))
            steps = [
                lambda: g.tensor_scalar(ve, k["mv"][:, :, 1], EPS_LN, None, ALU.add),
                lambda: g.tensor_tensor(y0, ve, mhalf[:, :], ALU.pow),
                lambda: g.tensor_tensor(a, y0, y0, ALU.mult),
                lambda: g.tensor_tensor(b_, a, ve, ALU.mult),
                lambda: g.tensor_scalar(a, b_, -0.5, 1.5, ALU.mult, ALU.add),
            ]
            wait_apart(g, k["var"], n * QT + QT)
            for i, step in enumerate(steps):
                step().then_inc(k["step"], 1)
                wait_apart(g, k["step"], n * len(steps) + i + 1)
            g.tensor_tensor(k["rstd"][:, :], y0, a, ALU.mult).then_inc(k["ready"], 1)

        def ln_apply(c, n, src, dst):
            k = norm[c]
            nc.vector.wait_ge(k["ready"], n + 1)
            for t in range(QT):
                nc.vector.tensor_scalar(dst(t), src(t), k["mv"][:, t, 0:1], k["rstd"][:, t:t + 1],
                                        ALU.subtract, ALU.mult).then_inc(k["out"], 1)

        @block.vector
        def _(dve):
            v = nc.vector
            v.memset(one[:, :], 1.0)
            v.memset(negc[:, 0:1], -0.5)
            v.memset(negc[:, 1:2], -0.625).then_inc(W.const_ready, 1)
            v.memset(vaug[:, :, :, :], 0.0).then_inc(W.const_ready, 1)
            dve.wait_ge(W.const_ready, 2)
            v.memset(vaug[:, :, :, DH:DH + 1], 1.0).then_inc(W.const_ready, 1)
            v.memset(qst, 0.0).then_inc(W.const_ready, 1)
            v.memset(kst, 1.0).then_inc(W.const_ready, 1)
            dve.wait_ge(W.w_loaded, 16 * 11)
            v.tensor_copy(identb[:, :], ident)
            v.tensor_copy(maskA[:, :], cst[:, C_MA:C_MA + P])
            v.tensor_copy(maskB[:, :], cst[:, C_MB:C_MB + P])
            v.tensor_scalar(bqs[:, :], col[:, V_BQ:V_BQ + 1], SCALE, None, ALU.mult).then_inc(W.const_ready, 1)
            v.tensor_copy(wins[:, 0, :], win[:, :]).then_inc(W.w_split, 1)
            dve.wait_ge(W.w_split, 1)
            v.tensor_tensor(win[:, :], win[:, :], wins[:, 0, :], ALU.subtract).then_inc(W.w_split, 1)
            dve.wait_ge(W.w_split, 2)
            v.tensor_copy(wins[:, 1, :], win[:, :]).then_inc(W.w_split, 1)
            dve.wait_ge(W.w_split, 3)
            v.tensor_tensor(wins[:, 2, :], win[:, :], wins[:, 1, :], ALU.subtract).then_inc(W.w_split, 1)

            def tile_of(b):
                return lambda t: xs[:, bass.ds(b * QT + t, 1), :].rearrange("p a d -> p (a d)")

            def batch_of(b):
                return xs[:, bass.ds(b * QT, QT), :]

            four = lambda a: a.rearrange("p (t d) -> p t d", t=QT)
            out_f, out_b = norm["f"]["out"], norm["b"]["out"]

            def stats0(f):
                wait_apart(dve, W.x_loaded, f * 16 + 16)
                ln_stats("f", f * 3, tile_of(f))

            def apply0(f):
                ln_apply("f", f * 3, tile_of(f), lambda t: hn[:, t, :])

            def split_h(f):
                dve.wait_ge(W.tr0, f + 1)
                v.tensor_scalar(hp[:, 0, :], X[:, :], GRID, GRID, ALU.add, ALU.subtract).then_inc(W.h_grid, 1)
                dve.wait_ge(W.h_grid, f + 1)
                v.tensor_tensor(hr, X[:, :], hp[:, 0, :], ALU.subtract).then_inc(W.h_rest, 1)

            def split_h3(f):
                dve.wait_ge(W.h_mid, f + 1)
                v.tensor_tensor(hp[:, 2, :], hr, hp[:, 1, :], ALU.subtract).then_inc(W.h_split, 1)

            def clip(f, z, evac, done):
                dve.wait_ge(evac, f + 1)
                v.tensor_scalar(z[0], z[0], -CLIP, CLIP, ALU.max, ALU.min).then_inc(done, 1)

            def odd_orders(f, z, sq, clipped, done):
                dve.wait_ge(sq, f * 3 + 3)
                dve.wait_ge(clipped, f + 1)
                v.scalar_tensor_tensor(z[2], z[1], -0.75, z[0], ALU.add, ALU.mult).then_inc(done, 1)
                v.scalar_tensor_tensor(z[4], z[4], -5 / 64, z[0], ALU.add, ALU.mult).then_inc(done, 1)

            def times_v(f):
                dve.wait_ge(W.hv_ev, f + 1)
                dve.wait_ge(W.k_t24, f * 2 + 2)
                dve.wait_ge(W.k_t35, f * 2 + 2)
                for p in range(ORDERS):
                    v.scalar_tensor_tensor(kv[:, p, :], kx[p], COEF[p], va[:, :], ALU.mult, ALU.mult).then_inc(W.kv_ready, 1)

            def running(out_, in_, done):
                v.tensor_tensor_scan(out_, one[:, 0:1].to_broadcast((P, T)), in_, 0.0, ALU.mult, ALU.add).then_inc(done, 1)

            def den_terms(f):
                dve.wait_ge(W.ks_mm, f + 1)
                running(ksum[:, :], X[:, :], W.k_scan)
                dve.wait_ge(W.qs_mm, f + 1)
                dve.wait_ge(W.k_scan, f + 1)
                v.tensor_tensor(ksum[:, :], Y[:, :], ksum[:, :], ALU.mult).then_inc(W.d_prod, 1)

            def sum_kv(f, orders):
                for p in orders:
                    dve.wait_ge(W.kv_ready, f * ORDERS + p + 1)
                    running(kv[:, p, :], kv[:, p, :], W.kv_sum)

            def invert_den(f):
                dve.wait_ge(W.den_mm, f + 1)
                v.tensor_scalar(den[:, :], X[:, 0:QT * H], EPS_DEN, None, ALU.add).then_inc(W.den_eps, 1)
                dve.wait_ge(W.den_eps, f + 1)
                v.reciprocal(den[:, :], den[:, :]).then_inc(W.den_rec, 1)

            def num(f):
                dve.wait_ge(W.qk_prod, f * ORDERS + ORDERS)
                for i, (o, a, c) in enumerate([(1, 0, 1), (3, 2, 3), (3, 3, 4), (1, 1, 3)]):
                    if i >= 2:
                        dve.wait_ge(W.n_add, f * 4 + i)
                    v.tensor_tensor(kv[:, o, :], kv[:, a, :], kv[:, c, :], ALU.add).then_inc(W.n_add, 1)

            def times_q(f):
                dve.wait_ge(W.q_t24, f * 2 + 2)
                dve.wait_ge(W.q_t35, f * 2 + 2)
                for p in range(ORDERS):
                    dve.wait_ge(W.kv_sum, f * ORDERS + p + 1)
                    v.tensor_tensor(kv[:, p, :], qx[p], kv[:, p, :], ALU.mult).then_inc(W.qk_prod, 1)

            def ratio(f):
                dve.wait_ge(W.n_add, f * 4 + 4)
                dve.wait_ge(W.rdB_mm, f + 1)
                v.tensor_tensor(outT[:, :], Y[:, :], kv[:, 1, :], ALU.mult).then_inc(W.outT_ready, 1)

            def add_x1(f):
                dve.wait_ge(W.o1_mm, f + 1)
                v.tensor_tensor(batch_of(f), four(X[:, :]), batch_of(f), ALU.add).then_inc(W.x1_ready, 1)
                wait_apart(dve, W.x1_ready, f + 1)

            def stats1(f):
                ln_stats("f", f * 3 + 1, tile_of(f))

            def apply1(f):
                if not isinstance(f, int):
                    dve.wait_ge(W.h_kept, f)
                ln_apply("f", f * 3 + 1, tile_of(f), lambda t: hs[:, t, :])
                wait_apart(dve, out_f, f * 12 + 8)

            def stats2(f):
                ln_stats("f", f * 3 + 2, lambda t: hs[:, t, :])

            def apply2(f):
                ln_apply("f", f * 3 + 2, lambda t: hs[:, t, :], lambda t: hn[:, t, :])

            def keep_v(f, back):
                dve.wait_ge(W.av_mm, f + 1)
                if back is not None:
                    dve.wait_ge(W.pr_used, back * TILES + TILES)
                for t in range(QT):
                    v.tensor_tensor(vaug[:, t, :, 0:DH], X[:, t * P:(t + 1) * P].rearrange("p (h d) -> p h d", h=H),
                                    row[:, R_BV:R_BV + D].rearrange("p (h d) -> p h d", h=H), ALU.add).then_inc(W.v_ready, 1)

            def third_parts(f):
                dve.wait_ge(W.p2_ready, f * 2 + 1)
                v.tensor_tensor(qs[:, 2, :], rq, qs[:, 1, :], ALU.subtract).then_inc(W.p3_ready, 1)
                dve.wait_ge(W.p2_ready, f * 2 + 2)
                v.tensor_tensor(ks[:, 2, :], rk, ks[:, 1, :], ALU.subtract).then_inc(W.p3_ready, 1)

            def maxima(f):
                for n in range(2 * H):
                    pair, t = n // QT, n % QT
                    dve.wait_ge(W.smax_mm, f * (2 * H) + n + 1)
                    v.tensor_reduce(nm[:, t * H + 2 * pair:t * H + 2 * pair + 2], ring[n % 2][:, :, 0:(t + 1) * P],
                                    AX.X, ALU.max, negate=True).then_inc(W.smax_red, 1)
                dve.wait_ge(W.n1_ready, f + 1)
                v.tensor_tensor(nmr[:, :], Z[0:QT * H, 0:P], nms[:, 0, :], ALU.subtract).then_inc(W.nr_ready, 1)
                dve.wait_ge(W.n2_ready, f + 1)
                v.tensor_tensor(nms[:, 2, :], nmr[:, :], nms[:, 1, :], ALU.subtract).then_inc(W.n3_ready, 1)

            def evacuate(b, g):
                dve.wait_ge(W.pr_used, b * TILES + 6 * (g + 1))
                v.tensor_copy(oT[:, g % 2, :], V[:, :]).then_inc(W.pv_ev, 1)

            def normalise(b, g):
                dve.wait_ge(W.ot_tr, b * 4 + g + 1)
                o4 = Z[:, :].rearrange("p (t j c) -> p t j c", t=QT, j=4)
                v.reciprocal(rec[:, :, :], o4[:, :, :, DH]).then_inc(W.rec_ready, 1)
                dve.wait_ge(W.rec_ready, b * 4 + g + 1)
                for t in range(QT):
                    v.tensor_tensor(y[:, t, 4 * g:4 * g + 4, :], o4[:, t, :, 0:DH],
                                    rec[:, t, :].unsqueeze(2).to_broadcast((P, 4, DH)), ALU.mult).then_inc(W.y_ready, 1)

            def x2(b):
                dve.wait_ge(W.o2_mm, b + 1)
                dve.wait_ge(W.h_kept, b + 1)
                v.tensor_tensor(hk[:, :, :], four(V[:, :]), hk[:, :, :], ALU.add).then_inc(W.x2a, 1)
                dve.wait_ge(W.x2a, b + 1)
                v.tensor_tensor(hk[:, :, :], hk[:, :, :], row[:, R_BP:R_BP + D].unsqueeze(1).to_broadcast((P, QT, D)),
                                ALU.add).then_inc(W.x2_ready, 1)
                wait_apart(dve, W.x2_ready, b + 1)
                ln_stats("b", b, lambda t: hk[:, t, :])
                v.tensor_tensor(batch_of(b), batch_of(b), hk[:, :, :], ALU.add).then_inc(W.xsum, 1)

            def apply3(b):
                ln_apply("b", b, lambda t: hk[:, t, :], lambda t: hb[:, t, :])

            def gate_top(b):
                dve.wait_ge(W.gate_mm, b + 1)
                v.tensor_tensor(lg[:, :, :], V[:, 0:QT * E].rearrange("p (t e) -> p t e", t=QT),
                                row[:, R_GB:R_GB + E].unsqueeze(1).to_broadcast((P, QT, E)), ALU.add).then_inc(W.lg_ready, 1)
                wait_apart(dve, W.lg_ready, b + 1)
                for t in range(QT):
                    v.max(top[:, t, :], lg[:, t, :]).then_inc(W.top_ready, 1)
                wait_apart(dve, W.top_ready, b * QT + QT)
                v.tensor_tensor(gt[:, 0, :], top[:, :, 1], top[:, :, 0], ALU.subtract).then_inc(W.g_step, 1)
                for t in range(QT):
                    v.max_index(topi[:, t, :], top[:, t, :], lg[:, t, :]).then_inc(W.topi_ready, 1)
                dve.wait_ge(W.topi_ready, b * QT + QT)
                v.tensor_copy(topf[:, :, :], topi[:, :, :]).then_inc(W.topf_ready, 1)

            def gate_weights(b):
                dve.wait_ge(W.g_exp, b + 1)
                v.tensor_scalar(gd[:, :], gt[:, 1, :], 1.0, None, ALU.add).then_inc(W.g_step, 1)
                dve.wait_ge(W.g_step, b * 4 + 2)
                v.reciprocal(gt[:, 2, :], gd[:, :]).then_inc(W.g_step, 1)
                dve.wait_ge(W.g_step, b * 4 + 3)
                v.tensor_tensor(gt[:, 3, :], gt[:, 1, :], gt[:, 2, :], ALU.mult).then_inc(W.g_step, 1)
                dve.wait_ge(W.topf_ready, b + 1)
                dve.wait_ge(W.g_step, b * 4 + 4)
                for t in range(QT):
                    for i in range(2):
                        v.tensor_scalar(oh[:, i, t, :], cst[:, C_IO:C_IO + E], topf[:, t, i:i + 1], gt[:, 2 + i, t:t + 1],
                                        ALU.is_equal, ALU.mult).then_inc(W.oh_ready, 1)
                dve.wait_ge(W.oh_ready, b * 2 * QT + 2 * QT)
                v.tensor_tensor(wf[:, :, :], oh[:, 0, :, :], oh[:, 1, :, :], ALU.add).then_inc(W.wf_ready, 1)
                dve.wait_ge(W.wf_ready, b + 1)
                v.tensor_copy(wfull[:, bass.ds(b * QT, QT), :], wf[:, :, :]).then_inc(W.wf_kept, 1)

            def add_b2(b):
                dve.wait_ge(W.b2_mm, b + 1)
                dve.wait_ge(W.xsum, b + 1)
                v.tensor_tensor(batch_of(b), four(V[:, :]), batch_of(b), ALU.add).then_inc(W.xb_ready, 1)

            def body(back, front):
                F_ = front is not None
                B_ = back is not None
                if F_:
                    stats0(front)
                    apply0(front)
                    split_h(front)
                if B_:
                    evacuate(back, 0)
                if F_:
                    split_h3(front)
                if B_:
                    normalise(back, 0)
                if F_:
                    clip(front, kx, W.hk_ev, W.k_clip)
                    clip(front, qx, W.hq_ev, W.q_clip)
                if B_:
                    evacuate(back, 1)
                if F_:
                    odd_orders(front, kx, W.k_sq, W.k_clip, W.k_t35)
                    odd_orders(front, qx, W.q_sq, W.q_clip, W.q_t35)
                if B_:
                    normalise(back, 1)
                if F_:
                    times_v(front)
                if B_:
                    evacuate(back, 2)
                if F_:
                    sum_kv(front, (0, 1))
                if B_:
                    normalise(back, 2)
                if F_:
                    den_terms(front)
                if B_:
                    evacuate(back, 3)
                if F_:
                    sum_kv(front, (2, 3))
                if B_:
                    normalise(back, 3)
                if F_:
                    sum_kv(front, (4,))
                    invert_den(front)
                    times_q(front)
                if B_:
                    x2(back)
                if F_:
                    num(front)
                if B_:
                    apply3(back)
                if F_:
                    ratio(front)
                    add_x1(front)
                    stats1(front)
                if B_:
                    gate_top(back)
                if F_:
                    apply1(front)
                    stats2(front)
                if B_:
                    gate_weights(back)
                if F_:
                    apply2(front)
                if B_:
                    add_b2(back)
                if F_:
                    keep_v(front, back)
                    third_parts(front)
                    maxima(front)

            pipelined(dve, body)

            dve.wait_ge(W.xb_ready, B)
            dve.wait_ge(W.wf_kept, B)
            dve.sem_inc(W.acc_ready, CREDIT * QT)
            with dve.Fori(0, B) as b:
                for e in range(E):
                    dve.wait_ge(W.y2_mm, b * E + e + 1 + CREDIT)
                    if e:
                        dve.wait_ge(W.acc_ready, b * (E * QT) + e * QT + CREDIT * QT)
                    for t in range(QT):
                        xt = xs[:, bass.ds(b * QT + t, 1), :].rearrange("p a d -> p (a d)")
                        v.scalar_tensor_tensor(xt, (Z, V)[e % 2][:, t * P:(t + 1) * P],
                                               wfull[:, bass.ds(b * QT + t, 1), e:e + 1].rearrange("p a d -> p (a d)"),
                                               xt, ALU.mult, ALU.add).then_inc(W.acc_ready, 1)

        @block.scalar
        def _(act):
            a = nc.scalar
            act.wait_ge(W.const_ready, 6)
            act.wait_ge(W.w_loaded, 16 * 11)

            def second_part(f):
                act.wait_ge(W.h_rest, f + 1)
                a.activation(hp[:, 1, :], hr, ACT.Copy).then_inc(W.h_mid, 1)

            def take_k(f):
                act.wait_ge(W.hk_mm, f + 1)
                a.activation(kx[0], Y[:, :], ACT.Copy, scale=SCALE).then_inc(W.hk_ev, 1)

            def take_q(f):
                act.wait_ge(W.hq_mm, f + 1)
                a.activation(qx[0], X[:, :], ACT.Copy, scale=SCALE).then_inc(W.hq_ev, 1)

            def take_v(f):
                act.wait_ge(W.hv_mm, f + 1)
                a.activation(va[:, :], Y[:, :], ACT.Copy).then_inc(W.hv_ev, 1)

            def square(f, z, clipped, sq):
                act.wait_ge(clipped, f + 1)
                a.activation(z[1], z[0], ACT.Square).then_inc(sq, 1)

            def squares(f, z, sq):
                act.wait_ge(sq, f * 3 + 1)
                a.activation(z[3], z[1], ACT.Square, bias=negc[:, 0:1]).then_inc(sq, 1)
                a.activation(z[4], z[1], ACT.Square, bias=negc[:, 1:2]).then_inc(sq, 1)

            def take_rden(f):
                act.wait_ge(W.rdT_mm, f + 1)
                a.activation(rdT[:, :], X[0:QT * H, P:2 * P], ACT.Copy).then_inc(W.rdT_ev, 1)

            def affine1(f):
                act.wait_ge(W.tr1, f + 1)
                a.activation(lnT[:, :], Y[:, :], ACT.Identity, bias=col[:, V_B1:V_B1 + 1],
                             scale=col[:, V_G1:V_G1 + 1]).then_inc(W.lnT_ready, 1)

            def take_qk(f):
                act.wait_ge(W.aq_mm, f + 1)
                a.activation(qf, X[:, :], ACT.Identity, bias=bqs[:, :], scale=SCALE).then_inc(W.qf_ready, 1)
                act.wait_ge(W.ak_mm, f + 1)
                a.activation(kf, Y[:, :], ACT.Identity, bias=col[:, V_BK:V_BK + 1]).then_inc(W.kf_ready, 1)
                act.wait_ge(W.qf_ready, f + 1)
                a.activation(qs[:, 0, :], qf, ACT.Copy).then_inc(W.p1_ready, 1)
                act.wait_ge(W.kf_ready, f + 1)
                a.activation(ks[:, 0, :], kf, ACT.Copy).then_inc(W.p1_ready, 1)
                act.wait_ge(W.r1_ready, f * 2 + 1)
                a.activation(qs[:, 1, :], rq, ACT.Copy).then_inc(W.p2_ready, 1)
                act.wait_ge(W.r1_ready, f * 2 + 2)
                a.activation(ks[:, 1, :], rk, ACT.Copy).then_inc(W.p2_ready, 1)

            def max_parts(f):
                act.wait_ge(W.nmT_mm, f + 1)
                a.activation(nms[:, 0, :], Z[0:QT * H, 0:P], ACT.Copy).then_inc(W.n1_ready, 1)
                act.wait_ge(W.nr_ready, f + 1)
                a.activation(nms[:, 1, :], nmr[:, :], ACT.Copy).then_inc(W.n2_ready, 1)

            def exps(b, n):
                width = T if n % 3 == 0 else T - P
                act.wait_ge(W.sc_mm, b * TILES + n + 1)
                if n >= PR:
                    act.wait_ge(W.pr_used, b * TILES + n - PR + 1)
                a.activation(pr[:, n % PR, :, 0:width], ring[n % 2][:, :, 0:width], ACT.Exp).then_inc(W.exp_ready, 1)

            def tail(b):
                act.wait_ge(W.yT_mm, b + 1)
                a.activation(yT[:, :], Z[:, :], ACT.Copy).then_inc(W.yT_ev, 1)

            def tail2(b):
                act.wait_ge(W.tr3, b + 1)
                a.activation(h2[:, :], Z[:, :], ACT.Identity, bias=col[:, V_B2:V_B2 + 1],
                             scale=col[:, V_G2:V_G2 + 1]).then_inc(W.h2_ready, 1)

            def tail3(b):
                act.wait_ge(W.g_step, b * 4 + 1)
                a.activation(gt[:, 1, :], gt[:, 0, :], ACT.Exp).then_inc(W.g_exp, 1)

            def tail4(b):
                act.wait_ge(W.wfT_mm, b + 1)
                a.activation(wfT[:, :, :], Z[0:E, :].rearrange("p (t n) -> p t n", t=QT), ACT.Copy).then_inc(W.wfT_ev, 1)

            def body(back, front):
                steps = {3: [second_part], 7: [take_k], 9: [take_q],
                         10: [take_v, lambda f: square(f, kx, W.k_clip, W.k_sq)], 11: [lambda f: squares(f, kx, W.k_sq)],
                         12: [lambda f: square(f, qx, W.q_clip, W.q_sq)], 13: [lambda f: squares(f, qx, W.q_sq)]}
                for n in range(TILES):
                    if back is not None:
                        exps(back, n)
                    if front is not None:
                        for step in steps.get(n, []):
                            step(front)
                if back is not None:
                    tail(back)
                if front is not None:
                    take_rden(front)
                if back is not None:
                    tail2(back)
                    tail3(back)
                    tail4(back)
                if front is not None:
                    affine1(front)
                    take_qk(front)
                    max_parts(front)
                if back is not None:
                    act.wait_ge(W.h2_kept, back * 16 + 16)

            pipelined(act, body)
            act.sem_inc(W.mid_ready, CREDIT)
            with act.Fori(0, B) as b:
                for n in range(E * HC):
                    e, c = n // HC, n % HC
                    act.wait_ge(W.mid_mm, b * (E * HC) + n + 1)
                    if c == 0:
                        act.wait_ge(W.y2_mm, b * E + e - 1 + CREDIT)
                    a.activation(hid[:, e % 2, c, :], (X, Y)[n % 2][:, :], ACT.Gelu,
                                 bias=col[:, V_EB + e * HC + c:V_EB + e * HC + c + 1]).then_inc(W.mid_ready, 1)

        @block.gpsimd
        def _(pool):
            g = nc.gpsimd
            g.memset(mhalf[:, :], -0.5).then_inc(W.pool_const, 1)
            pool.wait_ge(W.pool_const, 1)

            def even_orders(f, z, t35, done):
                wait_apart(pool, t35, f * 2 + 1)
                g.tensor_scalar(z[1], z[1], -0.5, None, ALU.add).then_inc(done, 1)
                g.tensor_scalar(z[3], z[3], -0.125, None, ALU.add).then_inc(done, 1)

            def body(back, front):
                if front is not None:
                    ln_rsqrt("f", front * 3)
                    even_orders(front, kx, W.k_t35, W.k_t24)
                    even_orders(front, qx, W.q_t35, W.q_t24)
                if back is not None:
                    ln_rsqrt("b", back)
                if front is not None:
                    ln_rsqrt("f", front * 3 + 1)
                    ln_rsqrt("f", front * 3 + 2)
                    pool.wait_ge(W.p1_ready, front * 2 + 1)
                    g.tensor_tensor(rq, qf, qs[:, 0, :], ALU.subtract).then_inc(W.r1_ready, 1)
                    pool.wait_ge(W.p1_ready, front * 2 + 2)
                    g.tensor_tensor(rk, kf, ks[:, 0, :], ALU.subtract).then_inc(W.r1_ready, 1)
                    if back is not None:
                        wait_apart(pool, norm["b"]["out"], back * QT + QT)
                        wait_apart(pool, W.xsum, back + 1)
                    g.tensor_copy(hk[:, :, :], hs[:, :, :]).then_inc(W.h_kept, 1)

            pipelined(pool, body)

        @block.tensor
        def _(pe):
            m = nc.tensor
            out_f, out_b = norm["f"]["out"], norm["b"]["out"]

            def turn(src, dst, done):
                for t in range(QT):
                    last = m.transpose(dst[:, t * P:(t + 1) * P], src(t), ident)
                last.then_inc(done, 1)

            pe.wait_ge(W.w_loaded, 16 * 11)
            pe.wait_ge(W.w_split, 4)
            pe.wait_ge(W.const_ready, 6)

            def turn_h(f):
                pe.wait_ge(out_f, f * 12 + 4)
                turn(lambda t: hn[:, t, :], X, W.tr0)

            def project(f, o, dst, done):
                terms = TERMS8 if o < 2 else TERMS6
                for i, (wi, hi) in enumerate(terms):
                    last = m.matmul(dst[:, :], wins[:, wi, o * D:(o + 1) * D], hp[:, hi, :],
                                    start=(i == 0), stop=(i == len(terms) - 1))
                last.then_inc(done, 1)

            def project_k(f):
                pe.wait_ge(W.h_split, f + 1)
                project(f, 1, Y, W.hk_mm)

            def project_q(f):
                project(f, 0, X, W.hq_mm)

            def project_v(f):
                pe.wait_ge(W.hk_ev, f + 1)
                project(f, 2, Y, W.hv_mm)

            def head_sums(f, z, dst, t24, t35, done, evacuated):
                pe.wait_ge(evacuated, f + 1)
                pe.wait_ge(t24, f * 2 + 2)
                pe.wait_ge(t35, f * 2 + 2)
                for p in range(ORDERS):
                    j, var = (p, 0) if p < 4 else (0, 1)
                    last = m.matmul(dst[32 * j:32 * j + 32, :], cst[:, C_SUM + 32 * var:C_SUM + 32 * var + 32], z[p],
                                    start=(p < 4), stop=(p > 0), skip_group_check=True)
                last.then_inc(done, 1)

            def denominators(f):
                pe.wait_ge(W.d_prod, f + 1)
                for t in range(QT):
                    last = m.matmul(X[:, t * H:(t + 1) * H], ksum[:, t * P:(t + 1) * P], cst[:, C_WS:C_WS + H],
                                    start=True, stop=True)
                last.then_inc(W.den_mm, 1)

            def turn_rden(f):
                wait_apart(pe, W.den_rec, f + 1)
                m.transpose(X[0:QT * H, P:2 * P], den[:, :], ident).then_inc(W.rdT_mm, 1)

            def spread_rden(f):
                pe.wait_ge(W.rdT_ev, f + 1)
                for t in range(QT):
                    last = m.matmul(Y[:, t * P:(t + 1) * P], cst[0:QT * H, C_SEL + P * t:C_SEL + P * (t + 1)], rdT[:, :],
                                    start=True, stop=True)
                last.then_inc(W.rdB_mm, 1)

            def output1(f):
                pe.wait_ge(W.outT_ready, f + 1)
                for t in range(QT):
                    last = m.matmul(X[:, t * P:(t + 1) * P], outT[:, t * P:(t + 1) * P], wo_sb[:, :], start=True, stop=True)
                last.then_inc(W.o1_mm, 1)

            def turn_ln(f):
                pe.wait_ge(out_f, f * 12 + 12)
                turn(lambda t: hn[:, t, :], Y, W.tr1)

            def project2(f):
                pe.wait_ge(W.lnT_ready, f + 1)
                m.matmul(X[:, :], wq_sb[:, :], lnT[:, :], start=True, stop=True).then_inc(W.aq_mm, 1)
                m.matmul(Y[:, :], wk_sb[:, :], lnT[:, :], start=True, stop=True).then_inc(W.ak_mm, 1)
                pe.wait_ge(W.qf_ready, f + 1)
                for t in range(QT):
                    last = m.matmul(X[:, t * P:(t + 1) * P], lnT[:, t * P:(t + 1) * P], wv_sb[:, :], start=True, stop=True)
                last.then_inc(W.av_mm, 1)

            def maxima(f):
                pe.wait_ge(W.stack_dma, f * (16 * 12) + 16 * 12)
                for n in range(2 * H):
                    pair, t = n // QT, n % QT
                    if n >= 2:
                        pe.wait_ge(W.smax_red, f * (2 * H) + n - 1)
                    for j in range(2):
                        h = 2 * pair + j
                        m.matmul(ring[n % 2][:, j, 0:(t + 1) * P], qst[0:MROW, h, t * P:(t + 1) * P], kst[0:MROW, h, 0:(t + 1) * P],
                                 start=True, stop=True)
                        last = m.matmul(ring[n % 2][:, j, t * P:(t + 1) * P], identb[:, :], maskA[:, :],
                                        start=False, stop=True, skip_group_check=True)
                    last.then_inc(W.smax_mm, 1)
                wait_apart(pe, W.smax_red, f * (2 * H) + 2 * H)
                m.transpose(Z[0:QT * H, 0:P], nm[:, :], ident).then_inc(W.nmT_mm, 1)

            def scores(b, n):
                if n == 0:
                    pe.wait_ge(W.max_dma, b * (16 * 12) + 16 * 12)
                else:
                    pe.wait_ge(W.exp_ready, b * TILES + max(n - 1, 1))
                for j in range(2):
                    h = 2 * (n // 3) + j
                    for t in ((0,), (1,), (2, 3))[n % 3]:
                        at = 2 * P if t == 3 else 0
                        dst = ring[n % 2][:, j, :]
                        m.matmul(dst[:, at:at + T - t * P], kst[0:MROW + 3, h, t * P:(t + 1) * P], qst[0:MROW + 3, h, t * P:T],
                                 start=True, stop=True)
                        last = m.matmul(dst[:, at:at + P], identb[:, :], maskB[:, :], start=False, stop=True, skip_group_check=True)
                last.then_inc(W.sc_mm, 1)

            def values(b, n):
                pe.wait_ge(W.exp_ready, b * TILES + n + 1)
                if n % 6 == 0 and n:
                    pe.wait_ge(W.pv_ev, b * 4 + n // 6)
                for j in range(2):
                    h = 2 * (n // 3) + j
                    r = 32 * (h % 4)
                    for t in ((0,), (1,), (2, 3))[n % 3]:
                        at = 2 * P if t == 3 else 0
                        last = m.matmul(V[r:r + 32, t * P:T], vaug[:, t, h, :], pr[:, n % PR, j, at:at + T - t * P],
                                        start=(t == 0), stop=(t == 3), skip_group_check=True)
                last.then_inc(W.pr_used, 1)

            def turn_back(b, g):
                pe.wait_ge(W.pv_ev, b * 4 + g + 1)
                if g:
                    pe.wait_ge(W.y_ready, b * 4 * QT + g * QT)
                turn(lambda t: oT[:, g % 2, t * P:(t + 1) * P], Z, W.ot_tr)

            def turn_y(b):
                pe.wait_ge(W.y_ready, b * 4 * QT + 4 * QT)
                turn(lambda t: yt[:, t, :], Z, W.yT_mm)

            def output2(b):
                pe.wait_ge(W.yT_ev, b + 1)
                for t in range(QT):
                    last = m.matmul(V[:, t * P:(t + 1) * P], yT[:, t * P:(t + 1) * P], wp_sb[:, :], start=True, stop=True)
                last.then_inc(W.o2_mm, 1)

            def turn_x2(b):
                pe.wait_ge(out_b, b * QT + QT)
                turn(lambda t: hb[:, t, :], Z, W.tr3)

            def gate(b):
                pe.wait_ge(W.h2_ready, b + 1)
                for t in range(QT):
                    last = m.matmul(V[:, t * E:(t + 1) * E], h2[:, t * P:(t + 1) * P], gw_sb[:, :], start=True, stop=True)
                last.then_inc(W.gate_mm, 1)

            def turn_weights(b):
                pe.wait_ge(W.wf_ready, b + 1)
                for t in range(QT):
                    last = m.transpose(Z[0:E, t * P:(t + 1) * P], wf[:, t, :], ident)
                last.then_inc(W.wfT_mm, 1)

            def bias2(b):
                pe.wait_ge(W.wfT_ev, b + 1)
                for t in range(QT):
                    last = m.matmul(V[:, t * P:(t + 1) * P], wfT[:, t, :], eb2_sb[:, :], start=True, stop=True)
                last.then_inc(W.b2_mm, 1)

            def body(back, front):
                steps = {3: [turn_h], 6: [project_k], 8: [project_q], 10: [project_v],
                         15: [lambda f: head_sums(f, kx, X, W.k_t24, W.k_t35, W.ks_mm, W.hq_ev)],
                         17: [lambda f: head_sums(f, qx, Y, W.q_t24, W.q_t35, W.qs_mm, W.hv_ev)],
                         22: [denominators]}
                if back is not None:
                    pe.wait_ge(W.v_ready, back * QT + QT)
                    scores(back, 0)
                for n in range(TILES):
                    if back is not None:
                        if n + 1 < TILES:
                            scores(back, n + 1)
                        values(back, n)
                        if n % 6 == 2 and n > 6:
                            turn_back(back, n // 6 - 1)
                    if front is not None:
                        for step in steps.get(n, []):
                            step(front)
                if back is not None:
                    turn_back(back, 3)
                if front is not None:
                    turn_rden(front)
                if back is not None:
                    turn_y(back)
                if front is not None:
                    spread_rden(front)
                if back is not None:
                    output2(back)
                if front is not None:
                    output1(front)
                if back is not None:
                    turn_x2(back)
                    gate(back)
                    turn_weights(back)
                    bias2(back)
                if front is not None:
                    turn_ln(front)
                    project2(front)
                if front is not None:
                    maxima(front)
                if back is not None:
                    pe.wait_ge(W.xb_ready, back + 1)

            pipelined(pe, body)

            pe.wait_ge(W.e_loaded, 16 * (1 + E))
            pe.wait_ge(W.xb_ready, B)
            pe.sem_inc(W.y2_mm, CREDIT)

            def hidden(b, e):
                for c in range(HC):
                    n = e * HC + c
                    pe.wait_ge(W.mid_ready, b * (E * HC) + n - 1 + CREDIT)
                    m.matmul((X, Y)[n % 2][:, :], w1_sb[:, e, c * P:(c + 1) * P],
                             h2c[:, bass.ds(b, 1), :].rearrange("p a n -> p (a n)"), start=True, stop=True).then_inc(W.mid_mm, 1)

            with pe.Fori(0, B) as b:
                pe.wait_ge(W.h2_loaded, b * 16 + 16)
                hidden(b, 0)
                for e in range(E):
                    if e + 1 < E:
                        hidden(b, e + 1)
                    pe.wait_ge(W.mid_ready, b * (E * HC) + (e + 1) * HC + CREDIT)
                    pe.wait_ge(W.acc_ready, b * (E * QT) + (e - 1) * QT + CREDIT * QT)
                    for t in range(QT):
                        for c in range(HC):
                            last = m.matmul((Z, V)[e % 2][:, t * P:(t + 1) * P], hid[:, e % 2, c, t * P:(t + 1) * P],
                                            w2_sb[:, e * HC + c, :], start=(c == 0), stop=(c == HC - 1))
                    last.then_inc(W.y2_mm, 1)


def kernel(**inputs):
    import numpy as _np
    import concourse.bacc as _bacc
    from concourse import mybir as _mybir
    from concourse.bass_utils import run_bass_kernel_spmd as _run

    a = {k: _np.asarray(v) for k, v in inputs.items()}
    f = lambda n: a["L0_ffn_" + n]
    by_width = lambda w: w.reshape(w.shape[:-1] + (H, DH)).swapaxes(-1, -2).reshape(w.shape)
    columns = _np.concatenate([_np.stack([f("ln1_g"), f("ln1_b"), f("ln2_g"), f("ln2_b"), by_width(f("bq")), by_width(f("bk"))], 1),
                               f("exp_b1").reshape(E * HC, P).T], 1)
    rows = _np.tile(_np.concatenate([f("bv"), f("bp"), f("gate_b")])[None], (P, 1))
    arrays = dict(x=a["L0_attn_x"], consts=constants(), cols=columns, rows=rows, w_in=a["L0_attn_W_in"].T,
                  w_out=a["L0_attn_W_out"].T, wq=by_width(f("Wq")), wk=by_width(f("Wk")), wv=f("Wv"), wp=f("Wp"), gate_w=f("gate_W"),
                  ew1=f("exp_W1"), ew2=f("exp_W2"), eb2=f("exp_b2"))
    arrays = {k: _np.ascontiguousarray(v) for k, v in arrays.items()}
    nc = _bacc.Bacc("TRN2", target_bir_lowering=False, num_devices=1)
    args = [nc.dram_tensor(f"in_{k}", v.shape, _mybir.dt.from_np(v.dtype), kind="ExternalInput").ap() for k, v in arrays.items()]
    out = nc.dram_tensor("out_0", (B, T, D), F32, kind="ExternalOutput").ap()
    block_kernel(nc, *args, out)
    r = _run(nc, [{f"in_{k}": v for k, v in arrays.items()}], core_ids=[0])
    return r.results[0]["out_0"]
```

```python
from contextlib import ExitStack

import numpy as np

import concourse.bass as bass
from concourse import mybir

F32 = mybir.dt.float32
BF16 = mybir.dt.bfloat16
U32 = mybir.dt.uint32
ALU = mybir.AluOpType
ACT = mybir.ActivationFunctionType
AX = mybir.AxisListType

P = 128
D = 128
B, T = 16, 512
QT = T // P
H, DH = 16, 8
E, HID = 8, 512
HC = HID // P
ORDERS = 5
EPS_LN = 1e-5
EPS_DEN = 1e-7
CLIP = float(np.float32(1.0) - np.float32(1e-6))
SCALE = float(np.float32(1.0) / np.sqrt(np.float32(DH)))
GRID = 1.5 * 2.0 ** 19
NEG = -1e30
TERMS8 = [(1, 2), (2, 1), (0, 2), (2, 0), (1, 1), (0, 1), (1, 0), (0, 0)]
TERMS6 = [(0, 2), (2, 0), (1, 1), (0, 1), (1, 0), (0, 0)]
PR = 4
CREDIT = 2
MROW = 96

C_ID, C_WS, C_SUM, C_SEL, C_MA, C_MB, C_IO = 0, 128, 144, 208, 720, 848, 976
C_N = 984
V_G1, V_B1, V_G2, V_B2, V_BQ, V_BK, V_EB = 0, 1, 2, 3, 4, 5, 6
V_N = V_EB + E * HC
R_BV, R_BP, R_GB = 0, 128, 256
R_N = 264


def beta():
    j = np.arange(6, dtype=np.float32)
    alpha = (j + 1.0) ** (-1.5)
    tail = np.flip(np.cumsum(np.flip(alpha)))
    b = np.concatenate([np.zeros(1, np.float32), tail[1:].astype(np.float32), np.zeros(5, np.float32)])
    return (b / b.sum()).astype(np.float32)


COEF = [float(beta()[p]) * 4.0 ** (p - 1) for p in range(1, ORDERS + 1)]


def constants():
    c = np.zeros((P, C_N), np.float32)
    i = np.arange(P)
    c[i, C_ID + i] = 1
    for h in range(H):
        for p in range(1, 5):
            c[32 * (p - 1) + h, C_WS + h] = COEF[p - 1]
        c[16 + h, C_WS + h] = COEF[4]
        c[DH * h:DH * h + DH, C_SUM + h] = 1
        c[DH * h:DH * h + DH, C_SUM + 32 + 16 + h] = 1
        for t in range(QT):
            c[H * t + h, C_SEL + P * t + DH * h:C_SEL + P * t + DH * h + DH] = 1
    c[:, C_MA:C_MA + P] = np.where(i[None, :] > i[:, None], NEG, 0)
    c[:, C_MB:C_MB + P] = np.where(i[:, None] > i[None, :], NEG, 0)
    c[:, C_IO:C_IO + E] = np.arange(E)
    return c


def block_kernel(nc, x, consts, cols, rows, w_in, w_out, wq, wk, wv, wp, gate_w, ew1, ew2, eb2, out):
    with ExitStack() as ctx:
        def sb(name, shape, dt=F32):
            return ctx.enter_context(nc.sbuf_tensor(name, shape, dt))

        def sem(name):
            return ctx.enter_context(nc.semaphore(name))

        xs = sb("xs", [P, B * QT, D])
        wfull = sb("wfull", [P, B * QT, E])
        w1_sb = sb("w1_sb", [P, E, HID])
        w2_sb = sb("w2_sb", [P, E * HC, D])
        cst = sb("cst", [P, C_N])
        col = sb("col", [P, V_N])
        row = sb("row", [P, R_N])
        win = sb("win", [P, 3 * D])
        wins = sb("wins", [P, 3, 3 * D], BF16)
        wo_sb = sb("wo_sb", [P, D])
        wq_sb = sb("wq_sb", [P, D])
        wk_sb = sb("wk_sb", [P, D])
        wv_sb = sb("wv_sb", [P, D])
        wp_sb = sb("wp_sb", [P, D])
        gw_sb = sb("gw_sb", [P, E])
        eb2_sb = sb("eb2_sb", [E, D])
        identb = sb("identb", [P, P], BF16)
        maskA = sb("maskA", [P, P], BF16)
        maskB = sb("maskB", [P, P], BF16)
        bqs = sb("bqs", [P, 1])
        one = sb("one", [P, 1])
        negc = sb("negc", [P, 2])
        mhalf = sb("mhalf", [P, QT])

        hn = sb("hn", [P, QT, D])
        ha = sb("ha", [P, QT, D])
        hs = sb("hs", [P, QT, D])
        hp = sb("hp", [P, 3, T], BF16)
        F = sb("F", [P, 10, T])
        kv = sb("kv", [P, ORDERS, T])
        va = sb("va", [P, T])
        ksum = sb("ksum", [P, T])
        outT = sb("outT", [P, T])
        den = sb("den", [P, QT * H])
        rdT = sb("rdT", [QT * H, P])
        qf = sb("qf", [P, T])
        kf = sb("kf", [P, T])
        lnT = sb("lnT", [P, T])
        qs = sb("qs", [P, 3, T], BF16)
        ks = sb("ks", [P, 3, T], BF16)
        nm = sb("nm", [P, H, QT])
        nms = sb("nms", [QT * H, 3, P], BF16)
        nmr = sb("nmr", [QT * H, P])
        stack = sb("stack", [P, 2, H, T], BF16)
        qst = stack[:, 0, :, :]
        kst = stack[:, 1, :, :]
        vaug = sb("vaug", [P, QT, H, 32])
        hk = sb("hk", [P, QT, D])
        pr = sb("pr", [P, PR, 2, T])
        oT = sb("oT", [P, 2, T])
        yt = sb("yt", [P, QT, D])
        yT = sb("yT", [P, T])
        rec = sb("rec", [P, QT, 4])
        h2 = sb("h2", [P, T])
        lg = sb("lg", [P, QT, E])
        top = sb("top", [P, QT, 8])
        topi = sb("topi", [P, QT, 8], U32)
        topf = sb("topf", [P, QT, 8])
        gt = sb("gt", [P, 4, QT])
        gd = sb("gd", [P, QT])
        oh = sb("oh", [P, 2, QT, E])
        wf = sb("wf", [P, QT, E])
        h2d = nc.dram_tensor("h2d", (B, P, T), F32, kind="Internal").ap()
        norm = {}
        for c in "amb":
            norm[c] = dict(st=sb("st" + c, [P, QT, 6]), mv=sb("mv" + c, [P, QT, 2]), lnv=sb("lnv" + c, [P, 4, QT]),
                           rstd=sb("rstd" + c, [P, QT]),
                           stats=sem("ln_stats_" + c), var=sem("ln_var_" + c), step=sem("ln_step_" + c),
                           ready=sem("ln_rstd_" + c), out=sem("ln_out_" + c))
        h2c = stack[:, :, :, :].rearrange("p a h n -> p (a h n)").bitcast(F32).rearrange("p (s n) -> p s n", n=T)
        hid = F[:, 0:8, :].rearrange("p (e c) n -> p e c n", e=2)

        qx, kx = [F[:, i, :] for i in range(5)], [F[:, 5 + i, :] for i in range(5)]
        hr = F[:, 9, :]
        y = yt[:, :, :].rearrange("p t (h d) -> p t h d", h=H)
        vb = lnT[:, :].rearrange("p (t d) -> p t d", t=QT)
        hb = yt
        wfT = yT[0:E, :].rearrange("e (t n) -> e t n", t=QT)
        ident = cst[:, C_ID:C_ID + P]

        X, Y, Z, V = (ctx.enter_context(nc.psum_tensor(n, [P, T], F32)) for n in ("front0", "front1", "back0", "back1"))
        ring = [ctx.enter_context(nc.psum_tensor(f"ring{i}", [P, 2, T], F32)) for i in range(2)]

        names = """w_loaded x_loaded e_loaded w_split const_ready pool_const
            tr0 h_grid h_rest h_mid h_split hq_mm hk_mm hv_mm hk_ev hq_ev hv_ev k_clip q_clip k_sq q_sq
            k_t35 q_t35 k_t24 q_t24 ks_mm qs_mm k_scan d_prod den_mm den_eps den_rec rdT_mm rdT_ev rdB_mm
            kv_ready kv_sum qk_prod n_add outT_ready o1_mm x1_ready tr1 lnT_ready aq_mm ak_mm av_mm
            qf_ready kf_ready v_ev p1_ready r1_ready p2_ready p3_ready v_ready stack_dma smax_mm smax_red
            nmT_mm n1_ready nr_ready n2_ready n3_ready max_dma h_kept sc_mm exp_ready pr_used pv_ev ot_tr
            rec_ready y_ready yT_mm yT_ev o2_mm x2a x2_ready xsum tr3 h2_ready h2_kept gate_mm lg_ready
            top_ready topi_ready topf_ready g_step g_exp oh_ready wf_ready wfT_mm wfT_ev b2_mm xb_ready
            wf_kept h2_loaded mid_mm mid_ready y2_mm acc_ready stored""".split()
        W = type("Sems", (), {n: sem(n) for n in names})
        TILES = 3 * H // 2
        STEPS = TILES // 2
        KEYS = ((0,), (1,), (2, 3))

        def wait_apart(engine, semaphore, value):
            engine.wait_ge(semaphore, value)
            engine.nop(nofuse=True)

        def pipelined(engine, body):
            body(None, None, 0)
            body(None, 0, 1)
            with engine.Fori(0, B - 2) as b:
                body(b, b + 1, b + 2)
            body(B - 2, B - 1, None)
            body(B - 1, None, None)

        block = ctx.enter_context(nc.Block())

        @block.sync
        def _(sp):
            loads = [(cst, consts), (col, cols), (row, rows), (win, w_in), (wo_sb, w_out), (wq_sb, wq),
                     (wk_sb, wk), (wv_sb, wv), (wp_sb, wp), (gw_sb, gate_w), (eb2_sb, eb2)]
            xv = x.rearrange("b (t p) d -> b p t d", p=P)

            def load_x(b):
                sp.dma_start(xs[:, bass.ds(b * QT, QT), :],
                             xv[bass.ds(b, 1), :, :, :].rearrange("a p t d -> (a p) t d")).then_inc(W.x_loaded, 16)

            load_x(0)
            for dst, src in loads:
                sp.dma_start(dst[:, :], src).then_inc(W.w_loaded, 16)
            sp.wait_ge(W.x_loaded, 16)
            with sp.Fori(1, B) as b:
                load_x(b)
                wait_apart(sp, W.x_loaded, b * 16 + 16)
            sp.dma_start(w1_sb[:, :, :], ew1.rearrange("e d n -> d e n")).then_inc(W.e_loaded, 16)
            for e in range(E):
                sp.dma_start(w2_sb[:, e * HC:(e + 1) * HC, :], ew2[e].rearrange("(c p) d -> p c d", p=P)).then_inc(W.e_loaded, 16)

            def body(b, m, f):
                if m is not None:
                    sp.wait_ge(W.p2_ready, m * 2 + 2)
                    sp.wait_ge(W.p3_ready, m * 2 + 2)
                    if b is not None:
                        sp.wait_ge(W.sc_mm, b * TILES + TILES)
                    for n, (i, j) in enumerate(TERMS6):
                        sp.dma_start(qst[DH * n:DH * n + DH, :, :], qs[:, i, :]).then_inc(W.stack_dma, 16)
                        sp.dma_start(kst[DH * n:DH * n + DH, :, :], ks[:, j, :]).then_inc(W.stack_dma, 16)
                if b is not None:
                    sp.wait_ge(W.h2_ready, b + 1)
                    sp.dma_start(h2d[bass.ds(b, 1), :, :].rearrange("a p n -> (a p) n"), h2[:, :]).then_inc(W.h2_kept, 16)
                if m is not None:
                    sp.wait_ge(W.n2_ready, m + 1)
                    sp.wait_ge(W.n3_ready, m + 1)
                    for i in range(3):
                        sp.dma_start(qst[MROW + i:MROW + i + 1, :, :], nms[:, i, :]).then_inc(W.max_dma, 16)

            pipelined(sp, body)
            sp.wait_ge(W.h2_kept, 16 * B)
            sp.wait_ge(W.sc_mm, B * TILES)
            ov = out.rearrange("b (t p) d -> b p t d", p=P)
            with sp.Fori(0, B) as b:
                sp.dma_start(h2c[:, bass.ds(b, 1), :].rearrange("p a n -> p (a n)"),
                             h2d[bass.ds(b, 1), :, :].rearrange("a p n -> (a p) n")).then_inc(W.h2_loaded, 16)
                wait_apart(sp, W.h2_loaded, b * 16 + 16)
            with sp.Fori(0, B) as b:
                sp.wait_ge(W.acc_ready, b * (E * QT) + E * QT + CREDIT * QT)
                sp.dma_start(ov[bass.ds(b, 1), :, :, :].rearrange("a p t d -> (a p) t d"), xs[:, bass.ds(b * QT, QT), :]).then_inc(W.stored, 16)
            sp.wait_ge(W.stored, 16 * B)

        def ln_stats(c, n, src):
            k = norm[c]
            for t in range(QT):
                nc.vector.bn_stats(k["st"][:, t, :], src(t)).then_inc(k["stats"], 1)
            wait_apart(nc.vector, k["stats"], n * QT + QT)
            for t in range(QT):
                nc.vector.bn_aggr(k["mv"][:, t, :], k["st"][:, t, :]).then_inc(k["var"], 1)

        def ln_rsqrt(c, n):
            g, k = nc.gpsimd, norm[c]
            ve, y0, a, b_ = (k["lnv"][:, i, :] for i in range(4))
            steps = [
                lambda: g.tensor_scalar(ve, k["mv"][:, :, 1], EPS_LN, None, ALU.add),
                lambda: g.tensor_tensor(y0, ve, mhalf[:, :], ALU.pow),
                lambda: g.tensor_tensor(a, y0, y0, ALU.mult),
                lambda: g.tensor_tensor(b_, a, ve, ALU.mult),
                lambda: g.tensor_scalar(a, b_, -0.5, 1.5, ALU.mult, ALU.add),
            ]
            wait_apart(g, k["var"], n * QT + QT)
            for i, step in enumerate(steps):
                step().then_inc(k["step"], 1)
                wait_apart(g, k["step"], n * len(steps) + i + 1)
            g.tensor_tensor(k["rstd"][:, :], y0, a, ALU.mult).then_inc(k["ready"], 1)

        def ln_apply(c, n, src, dst):
            k = norm[c]
            nc.vector.wait_ge(k["ready"], n + 1)
            for t in range(QT):
                nc.vector.tensor_scalar(dst(t), src(t), k["mv"][:, t, 0:1], k["rstd"][:, t:t + 1],
                                        ALU.subtract, ALU.mult).then_inc(k["out"], 1)

        @block.vector
        def _(dve):
            v = nc.vector
            v.memset(one[:, :], 1.0)
            v.memset(negc[:, 0:1], -0.5)
            v.memset(negc[:, 1:2], -0.625).then_inc(W.const_ready, 1)
            v.memset(vaug[:, :, :, :], 0.0).then_inc(W.const_ready, 1)
            dve.wait_ge(W.const_ready, 2)
            v.memset(vaug[:, :, :, DH:DH + 1], 1.0).then_inc(W.const_ready, 1)
            v.memset(qst, 0.0).then_inc(W.const_ready, 1)
            v.memset(kst, 1.0).then_inc(W.const_ready, 1)
            dve.wait_ge(W.w_loaded, 16 * 11)
            v.tensor_copy(identb[:, :], ident)
            v.tensor_copy(maskA[:, :], cst[:, C_MA:C_MA + P])
            v.tensor_copy(maskB[:, :], cst[:, C_MB:C_MB + P])
            v.tensor_scalar(bqs[:, :], col[:, V_BQ:V_BQ + 1], SCALE, None, ALU.mult).then_inc(W.const_ready, 1)
            v.tensor_copy(wins[:, 0, :], win[:, :]).then_inc(W.w_split, 1)
            dve.wait_ge(W.w_split, 1)
            v.tensor_tensor(win[:, :], win[:, :], wins[:, 0, :], ALU.subtract).then_inc(W.w_split, 1)
            dve.wait_ge(W.w_split, 2)
            v.tensor_copy(wins[:, 1, :], win[:, :]).then_inc(W.w_split, 1)
            dve.wait_ge(W.w_split, 3)
            v.tensor_tensor(wins[:, 2, :], win[:, :], wins[:, 1, :], ALU.subtract).then_inc(W.w_split, 1)

            def tile_of(b):
                return lambda t: xs[:, bass.ds(b * QT + t, 1), :].rearrange("p a d -> p (a d)")

            def batch_of(b):
                return xs[:, bass.ds(b * QT, QT), :]

            four = lambda a: a.rearrange("p (t d) -> p t d", t=QT)

            def stats0(f):
                wait_apart(dve, W.x_loaded, f * 16 + 16)
                ln_stats("a", f, tile_of(f))

            def apply0(f):
                ln_apply("a", f, tile_of(f), lambda t: hn[:, t, :])

            def split_h(f):
                dve.wait_ge(W.tr0, f + 1)
                v.tensor_scalar(hp[:, 0, :], X[:, :], GRID, GRID, ALU.add, ALU.subtract).then_inc(W.h_grid, 1)
                dve.wait_ge(W.h_grid, f + 1)
                v.tensor_tensor(hr, X[:, :], hp[:, 0, :], ALU.subtract).then_inc(W.h_rest, 1)

            def split_h3(f):
                dve.wait_ge(W.h_mid, f + 1)
                v.tensor_tensor(hp[:, 2, :], hr, hp[:, 1, :], ALU.subtract).then_inc(W.h_split, 1)

            def clip(f, z, evac, done):
                dve.wait_ge(evac, f + 1)
                v.tensor_scalar(z[0], z[0], -CLIP, CLIP, ALU.max, ALU.min).then_inc(done, 1)

            def odd_orders(f, z, sq, clipped, done):
                dve.wait_ge(sq, f * 3 + 3)
                dve.wait_ge(clipped, f + 1)
                v.scalar_tensor_tensor(z[2], z[1], -0.75, z[0], ALU.add, ALU.mult).then_inc(done, 1)
                v.scalar_tensor_tensor(z[4], z[4], -5 / 64, z[0], ALU.add, ALU.mult).then_inc(done, 1)

            def times_v(f):
                dve.wait_ge(W.hv_ev, f + 1)
                dve.wait_ge(W.k_t24, f * 2 + 2)
                dve.wait_ge(W.k_t35, f * 2 + 2)
                for p in range(ORDERS):
                    v.scalar_tensor_tensor(kv[:, p, :], kx[p], COEF[p], va[:, :], ALU.mult, ALU.mult).then_inc(W.kv_ready, 1)

            def running(out_, in_, done):
                v.tensor_tensor_scan(out_, one[:, 0:1].to_broadcast((P, T)), in_, 0.0, ALU.mult, ALU.add).then_inc(done, 1)

            def den_terms(f):
                dve.wait_ge(W.ks_mm, f + 1)
                running(ksum[:, :], X[:, :], W.k_scan)
                dve.wait_ge(W.qs_mm, f + 1)
                dve.wait_ge(W.k_scan, f + 1)
                v.tensor_tensor(ksum[:, :], Y[:, :], ksum[:, :], ALU.mult).then_inc(W.d_prod, 1)

            def sum_kv(f, orders):
                for p in orders:
                    dve.wait_ge(W.kv_ready, f * ORDERS + p + 1)
                    running(kv[:, p, :], kv[:, p, :], W.kv_sum)

            def invert_den(f):
                dve.wait_ge(W.den_mm, f + 1)
                v.tensor_scalar(den[:, :], X[:, 0:QT * H], EPS_DEN, None, ALU.add).then_inc(W.den_eps, 1)
                dve.wait_ge(W.den_eps, f + 1)
                v.reciprocal(den[:, :], den[:, :]).then_inc(W.den_rec, 1)

            def ratio(f):
                dve.wait_ge(W.n_add, f * 4 + 4)
                dve.wait_ge(W.rdB_mm, f + 1)
                v.tensor_tensor(outT[:, :], Y[:, :], kv[:, 1, :], ALU.mult).then_inc(W.outT_ready, 1)

            def add_x1(f):
                dve.wait_ge(W.o1_mm, f + 1)
                v.tensor_tensor(batch_of(f), four(X[:, :]), batch_of(f), ALU.add).then_inc(W.x1_ready, 1)
                wait_apart(dve, W.x1_ready, f + 1)

            def stats1(m):
                ln_stats("m", m * 2, tile_of(m))

            def apply1(m):
                if not isinstance(m, int) or m:
                    dve.wait_ge(W.h_kept, m)
                ln_apply("m", m * 2, tile_of(m), lambda t: hs[:, t, :])
                wait_apart(dve, norm["m"]["out"], m * 8 + 4)

            def stats2(m):
                ln_stats("m", m * 2 + 1, lambda t: hs[:, t, :])

            def apply2(m):
                ln_apply("m", m * 2 + 1, lambda t: hs[:, t, :], lambda t: ha[:, t, :])

            def keep_v(m, b):
                dve.wait_ge(W.v_ev, m + 1)
                if b is not None:
                    dve.wait_ge(W.pr_used, b * STEPS + STEPS)
                for t in range(QT):
                    v.tensor_tensor(vaug[:, t, :, 0:DH], vb[:, t, :].rearrange("p (h d) -> p h d", h=H),
                                    row[:, R_BV:R_BV + D].rearrange("p (h d) -> p h d", h=H), ALU.add).then_inc(W.v_ready, 1)

            def third_parts(m):
                dve.wait_ge(W.p2_ready, m * 2 + 1)
                v.tensor_tensor(qs[:, 2, :], qf[:, :], qs[:, 1, :], ALU.subtract).then_inc(W.p3_ready, 1)
                dve.wait_ge(W.p2_ready, m * 2 + 2)
                v.tensor_tensor(ks[:, 2, :], kf[:, :], ks[:, 1, :], ALU.subtract).then_inc(W.p3_ready, 1)

            def maximum(m, n):
                pair, t = n // QT, n % QT
                dve.wait_ge(W.smax_mm, m * (2 * H) + n + 1)
                v.tensor_reduce(nm[:, 2 * pair:2 * pair + 2, t], ring[n % 2][:, :, 0:(t + 1) * P],
                                AX.X, ALU.max, negate=True).then_inc(W.smax_red, 1)

            def max_rest(m):
                dve.wait_ge(W.n1_ready, m + 1)
                v.tensor_tensor(nmr[:, :], Z[0:QT * H, 0:P], nms[:, 0, :], ALU.subtract).then_inc(W.nr_ready, 1)
                dve.wait_ge(W.n2_ready, m + 1)
                v.tensor_tensor(nms[:, 2, :], nmr[:, :], nms[:, 1, :], ALU.subtract).then_inc(W.n3_ready, 1)

            def normalise(b, g):
                dve.wait_ge(W.ot_tr, b * 4 + g + 1)
                o4 = Z[:, :].rearrange("p (t j c) -> p t j c", t=QT, j=4)
                v.reciprocal(rec[:, :, :], o4[:, :, :, DH]).then_inc(W.rec_ready, 1)
                dve.wait_ge(W.rec_ready, b * 4 + g + 1)
                for t in range(QT):
                    v.tensor_tensor(y[:, t, 4 * g:4 * g + 4, :], o4[:, t, :, 0:DH],
                                    rec[:, t, :].unsqueeze(2).to_broadcast((P, 4, DH)), ALU.mult).then_inc(W.y_ready, 1)

            def x2(b):
                dve.wait_ge(W.o2_mm, b + 1)
                dve.wait_ge(W.h_kept, b + 1)
                v.tensor_tensor(hk[:, :, :], four(V[:, :]), hk[:, :, :], ALU.add).then_inc(W.x2a, 1)
                dve.wait_ge(W.x2a, b + 1)
                v.tensor_tensor(hk[:, :, :], hk[:, :, :], row[:, R_BP:R_BP + D].unsqueeze(1).to_broadcast((P, QT, D)),
                                ALU.add).then_inc(W.x2_ready, 1)
                wait_apart(dve, W.x2_ready, b + 1)
                ln_stats("b", b, lambda t: hk[:, t, :])

            def apply3(b):
                ln_apply("b", b, lambda t: hk[:, t, :], lambda t: hb[:, t, :])

            def gate_top(b):
                dve.wait_ge(W.gate_mm, b + 1)
                v.tensor_tensor(lg[:, :, :], V[:, 0:QT * E].rearrange("p (t e) -> p t e", t=QT),
                                row[:, R_GB:R_GB + E].unsqueeze(1).to_broadcast((P, QT, E)), ALU.add).then_inc(W.lg_ready, 1)
                wait_apart(dve, W.lg_ready, b + 1)
                for t in range(QT):
                    v.max(top[:, t, :], lg[:, t, :]).then_inc(W.top_ready, 1)
                wait_apart(dve, W.top_ready, b * QT + QT)
                v.tensor_tensor(gt[:, 0, :], top[:, :, 1], top[:, :, 0], ALU.subtract).then_inc(W.g_step, 1)
                for t in range(QT):
                    v.max_index(topi[:, t, :], top[:, t, :], lg[:, t, :]).then_inc(W.topi_ready, 1)
                dve.wait_ge(W.topi_ready, b * QT + QT)
                v.tensor_copy(topf[:, :, :], topi[:, :, :]).then_inc(W.topf_ready, 1)

            def gate_weights(b):
                dve.wait_ge(W.g_exp, b + 1)
                v.tensor_scalar(gd[:, :], gt[:, 1, :], 1.0, None, ALU.add).then_inc(W.g_step, 1)
                dve.wait_ge(W.g_step, b * 4 + 2)
                v.reciprocal(gt[:, 2, :], gd[:, :]).then_inc(W.g_step, 1)
                dve.wait_ge(W.g_step, b * 4 + 3)
                v.tensor_tensor(gt[:, 3, :], gt[:, 1, :], gt[:, 2, :], ALU.mult).then_inc(W.g_step, 1)
                dve.wait_ge(W.topf_ready, b + 1)
                dve.wait_ge(W.g_step, b * 4 + 4)
                for t in range(QT):
                    for i in range(2):
                        v.tensor_scalar(oh[:, i, t, :], cst[:, C_IO:C_IO + E], topf[:, t, i:i + 1], gt[:, 2 + i, t:t + 1],
                                        ALU.is_equal, ALU.mult).then_inc(W.oh_ready, 1)
                dve.wait_ge(W.oh_ready, b * 2 * QT + 2 * QT)
                v.tensor_tensor(wf[:, :, :], oh[:, 0, :, :], oh[:, 1, :, :], ALU.add).then_inc(W.wf_ready, 1)
                dve.wait_ge(W.wf_ready, b + 1)
                v.tensor_copy(wfull[:, bass.ds(b * QT, QT), :], wf[:, :, :]).then_inc(W.wf_kept, 1)

            def add_b2(b):
                dve.wait_ge(W.b2_mm, b + 1)
                dve.wait_ge(W.xsum, b + 1)
                v.tensor_tensor(batch_of(b), four(V[:, :]), batch_of(b), ALU.add).then_inc(W.xb_ready, 1)

            def body(b, m, f):
                last, middle, first = b is not None, m is not None, f is not None
                if middle:
                    stats1(m)
                if first:
                    stats0(f)
                if middle:
                    apply1(m)
                    stats2(m)
                if first:
                    apply0(f)
                if middle:
                    apply2(m)
                if first:
                    split_h(f)
                if last:
                    normalise(b, 0)
                if first:
                    split_h3(f)
                if last:
                    normalise(b, 1)
                if middle:
                    third_parts(m)
                if first:
                    clip(f, kx, W.hk_ev, W.k_clip)
                    clip(f, qx, W.hq_ev, W.q_clip)
                if last:
                    normalise(b, 2)
                if first:
                    odd_orders(f, kx, W.k_sq, W.k_clip, W.k_t35)
                    odd_orders(f, qx, W.q_sq, W.q_clip, W.q_t35)
                if last:
                    normalise(b, 3)
                if middle:
                    keep_v(m, b)
                for n in range(2 * H):
                    if middle:
                        maximum(m, n)
                    at = lambda place, stage: n == place and stage
                    if at(3, first):
                        times_v(f)
                    if at(5, last):
                        x2(b)
                    if at(7, first):
                        den_terms(f)
                    if at(8, first):
                        sum_kv(f, (0, 1, 2))
                    if at(9, last):
                        apply3(b)
                    if at(11, first):
                        sum_kv(f, (3, 4))
                    if at(12, first):
                        invert_den(f)
                    if at(16, last):
                        gate_top(b)
                    if at(19, last):
                        gate_weights(b)
                    if at(22, first):
                        ratio(f)
                    if at(25, last):
                        add_b2(b)
                    if at(27, first):
                        add_x1(f)
                if middle:
                    max_rest(m)

            pipelined(dve, body)

            dve.wait_ge(W.xb_ready, B)
            dve.wait_ge(W.wf_kept, B)
            dve.sem_inc(W.acc_ready, CREDIT * QT)
            with dve.Fori(0, B) as b:
                for e in range(E):
                    dve.wait_ge(W.y2_mm, b * E + e + 1 + CREDIT)
                    if e:
                        dve.wait_ge(W.acc_ready, b * (E * QT) + e * QT + CREDIT * QT)
                    for t in range(QT):
                        xt = xs[:, bass.ds(b * QT + t, 1), :].rearrange("p a d -> p (a d)")
                        v.scalar_tensor_tensor(xt, (Z, V)[e % 2][:, t * P:(t + 1) * P],
                                               wfull[:, bass.ds(b * QT + t, 1), e:e + 1].rearrange("p a d -> p (a d)"),
                                               xt, ALU.mult, ALU.add).then_inc(W.acc_ready, 1)

        @block.scalar
        def _(act):
            a = nc.scalar
            act.wait_ge(W.const_ready, 6)
            act.wait_ge(W.w_loaded, 16 * 11)

            def second_part(f):
                act.wait_ge(W.h_rest, f + 1)
                a.activation(hp[:, 1, :], hr, ACT.Copy).then_inc(W.h_mid, 1)

            def take_k(f):
                act.wait_ge(W.hk_mm, f + 1)
                a.activation(kx[0], Y[:, :], ACT.Copy, scale=SCALE).then_inc(W.hk_ev, 1)

            def take_q(f):
                act.wait_ge(W.hq_mm, f + 1)
                a.activation(qx[0], X[:, :], ACT.Copy, scale=SCALE).then_inc(W.hq_ev, 1)

            def take_v(f):
                act.wait_ge(W.hv_mm, f + 1)
                a.activation(va[:, :], Y[:, :], ACT.Copy).then_inc(W.hv_ev, 1)

            def square(f, z, clipped, sq):
                act.wait_ge(clipped, f + 1)
                a.activation(z[1], z[0], ACT.Square).then_inc(sq, 1)

            def squares(f, z, sq):
                act.wait_ge(sq, f * 3 + 1)
                a.activation(z[3], z[1], ACT.Square, bias=negc[:, 0:1]).then_inc(sq, 1)
                a.activation(z[4], z[1], ACT.Square, bias=negc[:, 1:2]).then_inc(sq, 1)

            def take_rden(f):
                act.wait_ge(W.rdT_mm, f + 1)
                a.activation(rdT[:, :], X[0:QT * H, P:2 * P], ACT.Copy).then_inc(W.rdT_ev, 1)

            def affine1(m):
                act.wait_ge(W.tr1, m + 1)
                a.activation(lnT[:, :], Y[:, :], ACT.Identity, bias=col[:, V_B1:V_B1 + 1],
                             scale=col[:, V_G1:V_G1 + 1]).then_inc(W.lnT_ready, 1)

            def take_qk(m):
                act.wait_ge(W.aq_mm, m + 1)
                a.activation(qf[:, :], X[:, :], ACT.Identity, bias=bqs[:, :], scale=SCALE).then_inc(W.qf_ready, 1)
                act.wait_ge(W.ak_mm, m + 1)
                a.activation(kf[:, :], Y[:, :], ACT.Identity, bias=col[:, V_BK:V_BK + 1]).then_inc(W.kf_ready, 1)
                act.wait_ge(W.qf_ready, m + 1)
                a.activation(qs[:, 0, :], qf[:, :], ACT.Copy).then_inc(W.p1_ready, 1)
                act.wait_ge(W.kf_ready, m + 1)
                a.activation(ks[:, 0, :], kf[:, :], ACT.Copy).then_inc(W.p1_ready, 1)

            def take_v2(m):
                act.wait_ge(W.av_mm, m + 1)
                a.activation(vb[:, :, :], X[:, :].rearrange("p (t d) -> p t d", t=QT), ACT.Copy).then_inc(W.v_ev, 1)

            def second_parts(m):
                act.wait_ge(W.r1_ready, m * 2 + 1)
                a.activation(qs[:, 1, :], qf[:, :], ACT.Copy).then_inc(W.p2_ready, 1)
                act.wait_ge(W.r1_ready, m * 2 + 2)
                a.activation(ks[:, 1, :], kf[:, :], ACT.Copy).then_inc(W.p2_ready, 1)

            def max_parts(f):
                act.wait_ge(W.nmT_mm, f + 1)
                a.activation(nms[:, 0, :], Z[0:QT * H, 0:P], ACT.Copy).then_inc(W.n1_ready, 1)
                act.wait_ge(W.nr_ready, f + 1)
                a.activation(nms[:, 1, :], nmr[:, :], ACT.Copy).then_inc(W.n2_ready, 1)

            def exps(b, n):
                width = T if (n // 2) % 3 == 0 else T - P
                act.wait_ge(W.sc_mm, b * TILES + n + 1)
                if n >= PR:
                    act.wait_ge(W.pr_used, b * STEPS + (n - PR) // 2 + 1)
                a.activation(pr[:, n % PR, :, 0:width], ring[n % 2][:, :, 0:width], ACT.Exp).then_inc(W.exp_ready, 1)

            def evacuate(b, g):
                act.wait_ge(W.pr_used, b * STEPS + 3 * (g + 1))
                a.activation(oT[:, g % 2, :], V[:, :], ACT.Copy).then_inc(W.pv_ev, 1)

            def tail(b):
                act.wait_ge(W.yT_mm, b + 1)
                a.activation(yT[:, :], Z[:, :], ACT.Copy).then_inc(W.yT_ev, 1)

            def tail2(b):
                act.wait_ge(W.tr3, b + 1)
                a.activation(h2[:, :], Z[:, :], ACT.Identity, bias=col[:, V_B2:V_B2 + 1],
                             scale=col[:, V_G2:V_G2 + 1]).then_inc(W.h2_ready, 1)

            def tail3(b):
                act.wait_ge(W.g_step, b * 4 + 1)
                a.activation(gt[:, 1, :], gt[:, 0, :], ACT.Exp).then_inc(W.g_exp, 1)

            def tail4(b):
                act.wait_ge(W.wfT_mm, b + 1)
                a.activation(wfT[:, :, :], Z[0:E, :].rearrange("p (t n) -> p t n", t=QT), ACT.Copy).then_inc(W.wfT_ev, 1)

            def body(b, m, f):
                last, middle, first = b is not None, m is not None, f is not None
                for n in range(TILES):
                    if last:
                        exps(b, n)
                        if n % 6 == 1 and n > 6:
                            evacuate(b, n // 6 - 1)
                    at = lambda place, stage: n == place and stage
                    if at(8, first):
                        second_part(f)
                    if at(10, middle):
                        affine1(m)
                    if at(13, middle):
                        take_qk(m)
                        take_v2(m)
                    if at(16, middle):
                        second_parts(m)
                    if at(19, first):
                        take_k(f)
                    if at(21, first):
                        take_q(f)
                if last:
                    evacuate(b, 3)
                if first:
                    take_v(f)
                    square(f, kx, W.k_clip, W.k_sq)
                    squares(f, kx, W.k_sq)
                    square(f, qx, W.q_clip, W.q_sq)
                    squares(f, qx, W.q_sq)
                if last:
                    tail(b)
                    tail2(b)
                if first:
                    take_rden(f)
                if last:
                    tail3(b)
                    tail4(b)
                if middle:
                    max_parts(m)
                if last:
                    act.wait_ge(W.h2_kept, b * 16 + 16)

            pipelined(act, body)
            act.sem_inc(W.mid_ready, CREDIT)
            with act.Fori(0, B) as b:
                for n in range(E * HC):
                    e, c = n // HC, n % HC
                    act.wait_ge(W.mid_mm, b * (E * HC) + n + 1)
                    if c == 0:
                        act.wait_ge(W.y2_mm, b * E + e - 1 + CREDIT)
                    a.activation(hid[:, e % 2, c, :], (X, Y)[n % 2][:, :], ACT.Gelu,
                                 bias=col[:, V_EB + e * HC + c:V_EB + e * HC + c + 1]).then_inc(W.mid_ready, 1)

        @block.gpsimd
        def _(pool):
            g = nc.gpsimd
            g.memset(mhalf[:, :], -0.5).then_inc(W.pool_const, 1)
            pool.wait_ge(W.pool_const, 1)

            def even_orders(f, z, t35, done):
                wait_apart(pool, t35, f * 2 + 1)
                g.tensor_scalar(z[1], z[1], -0.5, None, ALU.add).then_inc(done, 1)
                g.tensor_scalar(z[3], z[3], -0.125, None, ALU.add).then_inc(done, 1)

            def times_q(f):
                pool.wait_ge(W.q_t24, f * 2 + 2)
                pool.wait_ge(W.q_t35, f * 2 + 2)
                for p in range(ORDERS):
                    pool.wait_ge(W.kv_sum, f * ORDERS + p + 1)
                    g.tensor_tensor(kv[:, p, :], qx[p], kv[:, p, :], ALU.mult).then_inc(W.qk_prod, 1)
                for i, (o, a, c) in enumerate([(1, 0, 1), (3, 2, 3), (3, 3, 4), (1, 1, 3)]):
                    if i < 2:
                        pool.wait_ge(W.qk_prod, f * ORDERS + (2, 4)[i])
                    else:
                        pool.wait_ge(W.qk_prod, f * ORDERS + ORDERS)
                        pool.wait_ge(W.n_add, f * 4 + i)
                    g.tensor_tensor(kv[:, o, :], kv[:, a, :], kv[:, c, :], ALU.add).then_inc(W.n_add, 1)

            def body(b, m, f):
                last, middle, first = b is not None, m is not None, f is not None
                if middle:
                    ln_rsqrt("m", m * 2)
                if first:
                    ln_rsqrt("a", f)
                if middle:
                    ln_rsqrt("m", m * 2 + 1)
                    pool.wait_ge(W.p1_ready, m * 2 + 1)
                    g.tensor_tensor(qf[:, :], qf[:, :], qs[:, 0, :], ALU.subtract).then_inc(W.r1_ready, 1)
                    pool.wait_ge(W.p1_ready, m * 2 + 2)
                    g.tensor_tensor(kf[:, :], kf[:, :], ks[:, 0, :], ALU.subtract).then_inc(W.r1_ready, 1)
                if first:
                    even_orders(f, kx, W.k_t35, W.k_t24)
                    even_orders(f, qx, W.q_t35, W.q_t24)
                if last:
                    ln_rsqrt("b", b)
                    xb = xs[:, bass.ds(b * QT, QT), :]
                    wait_apart(pool, W.x2_ready, b + 1)
                    g.tensor_tensor(xb, xb, hk[:, :, :], ALU.add).then_inc(W.xsum, 1)
                if first:
                    times_q(f)
                if middle:
                    if last:
                        wait_apart(pool, norm["b"]["out"], b * QT + QT)
                        wait_apart(pool, W.xsum, b + 1)
                    wait_apart(pool, norm["m"]["out"], m * 8 + 8)
                    g.tensor_copy(hk[:, :, :], hs[:, :, :]).then_inc(W.h_kept, 1)

            pipelined(pool, body)

        @block.tensor
        def _(pe):
            k = nc.tensor

            def turn(src, dst, done):
                for t in range(QT):
                    last = k.transpose(dst[:, t * P:(t + 1) * P], src(t), ident)
                last.then_inc(done, 1)

            pe.wait_ge(W.w_loaded, 16 * 11)
            pe.wait_ge(W.w_split, 4)
            pe.wait_ge(W.const_ready, 6)

            def turn_h(f):
                pe.wait_ge(norm["a"]["out"], f * QT + QT)
                if not isinstance(f, int) or f:
                    pe.wait_ge(W.x1_ready, f)
                turn(lambda t: hn[:, t, :], X, W.tr0)

            def project(f, o, dst, done):
                terms = TERMS8 if o < 2 else TERMS6
                for i, (wi, hi) in enumerate(terms):
                    last = k.matmul(dst[:, :], wins[:, wi, o * D:(o + 1) * D], hp[:, hi, :],
                                    start=(i == 0), stop=(i == len(terms) - 1))
                last.then_inc(done, 1)

            def project_k(f, m):
                pe.wait_ge(W.h_split, f + 1)
                if m is not None:
                    pe.wait_ge(W.kf_ready, m + 1)
                project(f, 1, Y, W.hk_mm)

            def project_q(f, m):
                if m is not None:
                    pe.wait_ge(W.v_ev, m + 1)
                project(f, 0, X, W.hq_mm)

            def project_v(f):
                pe.wait_ge(W.hk_ev, f + 1)
                project(f, 2, Y, W.hv_mm)

            def head_sums(f, z, dst, t24, t35, done, evacuated):
                pe.wait_ge(evacuated, f + 1)
                pe.wait_ge(t24, f * 2 + 2)
                pe.wait_ge(t35, f * 2 + 2)
                for p in range(ORDERS):
                    j, var = (p, 0) if p < 4 else (0, 1)
                    last = k.matmul(dst[32 * j:32 * j + 32, :], cst[:, C_SUM + 32 * var:C_SUM + 32 * var + 32], z[p],
                                    start=(p < 4), stop=(p > 0), skip_group_check=True)
                last.then_inc(done, 1)

            def denominators(f):
                pe.wait_ge(W.d_prod, f + 1)
                for t in range(QT):
                    last = k.matmul(X[:, t * H:(t + 1) * H], ksum[:, t * P:(t + 1) * P], cst[:, C_WS:C_WS + H],
                                    start=True, stop=True)
                last.then_inc(W.den_mm, 1)

            def turn_rden(f):
                wait_apart(pe, W.den_rec, f + 1)
                k.transpose(X[0:QT * H, P:2 * P], den[:, :], ident).then_inc(W.rdT_mm, 1)

            def spread_rden(f):
                pe.wait_ge(W.rdT_ev, f + 1)
                for t in range(QT):
                    last = k.matmul(Y[:, t * P:(t + 1) * P], cst[0:QT * H, C_SEL + P * t:C_SEL + P * (t + 1)], rdT[:, :],
                                    start=True, stop=True)
                last.then_inc(W.rdB_mm, 1)

            def output1(f):
                pe.wait_ge(W.outT_ready, f + 1)
                for t in range(QT):
                    last = k.matmul(X[:, t * P:(t + 1) * P], outT[:, t * P:(t + 1) * P], wo_sb[:, :], start=True, stop=True)
                last.then_inc(W.o1_mm, 1)

            def turn_ln(m):
                pe.wait_ge(norm["m"]["out"], m * 8 + 8)
                turn(lambda t: ha[:, t, :], Y, W.tr1)

            def project2(m, f):
                pe.wait_ge(W.lnT_ready, m + 1)
                if f is not None:
                    pe.wait_ge(W.h_rest, f + 1)
                k.matmul(X[:, :], wq_sb[:, :], lnT[:, :], start=True, stop=True).then_inc(W.aq_mm, 1)
                k.matmul(Y[:, :], wk_sb[:, :], lnT[:, :], start=True, stop=True).then_inc(W.ak_mm, 1)
                pe.wait_ge(W.qf_ready, m + 1)
                for t in range(QT):
                    last = k.matmul(X[:, t * P:(t + 1) * P], lnT[:, t * P:(t + 1) * P], wv_sb[:, :], start=True, stop=True)
                last.then_inc(W.av_mm, 1)

            def maximum(m, n):
                pair, t = n // QT, n % QT
                if n == 0:
                    pe.wait_ge(W.stack_dma, m * (16 * 12) + 16 * 12)
                if n >= 2:
                    pe.wait_ge(W.smax_red, m * (2 * H) + n - 1)
                for j in range(2):
                    h = 2 * pair + j
                    k.matmul(ring[n % 2][:, j, 0:(t + 1) * P], qst[0:MROW, h, t * P:(t + 1) * P], kst[0:MROW, h, 0:(t + 1) * P],
                             start=True, stop=True)
                    last = k.matmul(ring[n % 2][:, j, t * P:(t + 1) * P], identb[:, :], maskA[:, :],
                                    start=False, stop=True, skip_group_check=True)
                last.then_inc(W.smax_mm, 1)

            def turn_maxima(m):
                wait_apart(pe, W.smax_red, m * (2 * H) + 2 * H)
                k.transpose(Z[0:QT * H, 0:P], nm[:, :, :].rearrange("p h t -> p (h t)"), ident).then_inc(W.nmT_mm, 1)

            def scores(b, n):
                if n == 0:
                    pe.wait_ge(W.max_dma, b * (16 * 3) + 16 * 3)
                else:
                    pe.wait_ge(W.exp_ready, b * TILES + max(n - 1, 1))
                for j in range(2):
                    h = 4 * (n // 6) + 2 * (n % 2) + j
                    for t in KEYS[(n // 2) % 3]:
                        at = 2 * P if t == 3 else 0
                        dst = ring[n % 2][:, j, :]
                        k.matmul(dst[:, at:at + T - t * P], kst[0:MROW + 3, h, t * P:(t + 1) * P], qst[0:MROW + 3, h, t * P:T],
                                 start=True, stop=True)
                        last = k.matmul(dst[:, at:at + P], identb[:, :], maskB[:, :], start=False, stop=True, skip_group_check=True)
                last.then_inc(W.sc_mm, 1)

            def values(b, s_):
                pe.wait_ge(W.exp_ready, b * TILES + 2 * s_ + 2)
                if s_ % 3 == 0 and s_:
                    pe.wait_ge(W.pv_ev, b * 4 + s_ // 3)
                for t in KEYS[s_ % 3]:
                    at = 2 * P if t == 3 else 0
                    for i in range(4):
                        n = 2 * s_ + i // 2
                        last = k.matmul(V[32 * i:32 * i + 32, t * P:T], vaug[:, t, 4 * (s_ // 3) + i, :],
                                        pr[:, n % PR, i % 2, at:at + T - t * P],
                                        start=(t == 0), stop=(t == 3), skip_group_check=True)
                last.then_inc(W.pr_used, 1)

            def turn_back(b, g):
                pe.wait_ge(W.pv_ev, b * 4 + g + 1)
                if g:
                    pe.wait_ge(W.y_ready, b * 4 * QT + g * QT)
                turn(lambda t: oT[:, g % 2, t * P:(t + 1) * P], Z, W.ot_tr)

            def turn_y(b):
                pe.wait_ge(W.y_ready, b * 4 * QT + 4 * QT)
                turn(lambda t: yt[:, t, :], Z, W.yT_mm)

            def output2(b):
                pe.wait_ge(W.yT_ev, b + 1)
                for t in range(QT):
                    last = k.matmul(V[:, t * P:(t + 1) * P], yT[:, t * P:(t + 1) * P], wp_sb[:, :], start=True, stop=True)
                last.then_inc(W.o2_mm, 1)

            def turn_x2(b):
                pe.wait_ge(norm["b"]["out"], b * QT + QT)
                turn(lambda t: hb[:, t, :], Z, W.tr3)

            def gate(b):
                pe.wait_ge(W.h2_ready, b + 1)
                for t in range(QT):
                    last = k.matmul(V[:, t * E:(t + 1) * E], h2[:, t * P:(t + 1) * P], gw_sb[:, :], start=True, stop=True)
                last.then_inc(W.gate_mm, 1)

            def turn_weights(b):
                pe.wait_ge(W.wf_ready, b + 1)
                for t in range(QT):
                    last = k.transpose(Z[0:E, t * P:(t + 1) * P], wf[:, t, :], ident)
                last.then_inc(W.wfT_mm, 1)

            def bias2(b):
                pe.wait_ge(W.wfT_ev, b + 1)
                for t in range(QT):
                    last = k.matmul(V[:, t * P:(t + 1) * P], wfT[:, t, :], eb2_sb[:, :], start=True, stop=True)
                last.then_inc(W.b2_mm, 1)

            def body(b, m, f):
                last, middle, first = b is not None, m is not None, f is not None
                if last:
                    pe.wait_ge(W.v_ready, b * QT + QT)
                    scores(b, 0)
                    scores(b, 1)
                for n in range(STEPS):
                    if last:
                        if n + 1 < STEPS:
                            scores(b, 2 * n + 2)
                            scores(b, 2 * n + 3)
                        values(b, n)
                        if n % 3 == 1 and n > 3:
                            turn_back(b, n // 3 - 1)
                    at = lambda place, stage: n == place and stage
                    if at(3, first):
                        turn_h(f)
                    if at(4, middle):
                        turn_ln(m)
                    if at(6, middle):
                        project2(m, f)
                    if at(8, first):
                        project_k(f, m)
                    if at(9, first):
                        project_q(f, m)
                    if at(10, first):
                        project_v(f)
                if last:
                    turn_back(b, 3)
                for n in range(2 * H):
                    if middle:
                        maximum(m, n)
                    at = lambda place, stage: n == place and stage
                    if at(0, last):
                        turn_y(b)
                    if at(2, last):
                        output2(b)
                    if at(4, first):
                        head_sums(f, kx, X, W.k_t24, W.k_t35, W.ks_mm, W.hq_ev)
                    if at(6, first):
                        head_sums(f, qx, Y, W.q_t24, W.q_t35, W.qs_mm, W.hv_ev)
                    if at(9, first):
                        denominators(f)
                    if at(11, last):
                        turn_x2(b)
                    if at(13, first):
                        turn_rden(f)
                    if at(14, last):
                        gate(b)
                    if at(15, first):
                        spread_rden(f)
                    if at(21, last):
                        turn_weights(b)
                    if at(23, last):
                        bias2(b)
                    if at(24, first):
                        output1(f)
                if middle:
                    turn_maxima(m)
                if last:
                    pe.wait_ge(W.xb_ready, b + 1)

            pipelined(pe, body)

            pe.wait_ge(W.e_loaded, 16 * (1 + E))
            pe.wait_ge(W.xb_ready, B)
            pe.sem_inc(W.y2_mm, CREDIT)

            def hidden(b, e):
                for c in range(HC):
                    n = e * HC + c
                    pe.wait_ge(W.mid_ready, b * (E * HC) + n - 1 + CREDIT)
                    k.matmul((X, Y)[n % 2][:, :], w1_sb[:, e, c * P:(c + 1) * P],
                             h2c[:, bass.ds(b, 1), :].rearrange("p a n -> p (a n)"), start=True, stop=True).then_inc(W.mid_mm, 1)

            with pe.Fori(0, B) as b:
                pe.wait_ge(W.h2_loaded, b * 16 + 16)
                hidden(b, 0)
                for e in range(E):
                    if e + 1 < E:
                        hidden(b, e + 1)
                    pe.wait_ge(W.mid_ready, b * (E * HC) + (e + 1) * HC + CREDIT)
                    pe.wait_ge(W.acc_ready, b * (E * QT) + (e - 1) * QT + CREDIT * QT)
                    for t in range(QT):
                        for c in range(HC):
                            last = k.matmul((Z, V)[e % 2][:, t * P:(t + 1) * P], hid[:, e % 2, c, t * P:(t + 1) * P],
                                            w2_sb[:, e * HC + c, :], start=(c == 0), stop=(c == HC - 1))
                    last.then_inc(W.y2_mm, 1)


def kernel(**inputs):
    import numpy as _np
    import concourse.bacc as _bacc
    from concourse import mybir as _mybir
    from concourse.bass_utils import run_bass_kernel_spmd as _run

    a = {k: _np.asarray(v) for k, v in inputs.items()}
    f = lambda n: a["L0_ffn_" + n]
    by_width = lambda w: w.reshape(w.shape[:-1] + (H, DH)).swapaxes(-1, -2).reshape(w.shape)
    columns = _np.concatenate([_np.stack([f("ln1_g"), f("ln1_b"), f("ln2_g"), f("ln2_b"), by_width(f("bq")), by_width(f("bk"))], 1),
                               f("exp_b1").reshape(E * HC, P).T], 1)
    rows = _np.tile(_np.concatenate([f("bv"), f("bp"), f("gate_b")])[None], (P, 1))
    arrays = dict(x=a["L0_attn_x"], consts=constants(), cols=columns, rows=rows, w_in=a["L0_attn_W_in"].T,
                  w_out=a["L0_attn_W_out"].T, wq=by_width(f("Wq")), wk=by_width(f("Wk")), wv=f("Wv"), wp=f("Wp"), gate_w=f("gate_W"),
                  ew1=f("exp_W1"), ew2=f("exp_W2"), eb2=f("exp_b2"))
    arrays = {k: _np.ascontiguousarray(v) for k, v in arrays.items()}
    nc = _bacc.Bacc("TRN2", target_bir_lowering=False, num_devices=1)
    args = [nc.dram_tensor(f"in_{k}", v.shape, _mybir.dt.from_np(v.dtype), kind="ExternalInput").ap() for k, v in arrays.items()]
    out = nc.dram_tensor("out_0", (B, T, D), F32, kind="ExternalOutput").ap()
    block_kernel(nc, *args, out)
    r = _run(nc, [{f"in_{k}": v for k, v in arrays.items()}], core_ids=[0])
    return r.results[0]["out_0"]
```

```python
from contextlib import ExitStack

import numpy as np

import concourse.bass as bass
from concourse import mybir

F32 = mybir.dt.float32
BF16 = mybir.dt.bfloat16
F32R = mybir.dt.float32r
U32 = mybir.dt.uint32
ALU = mybir.AluOpType
ACT = mybir.ActivationFunctionType
AX = mybir.AxisListType

P = 128
D = 128
B, T = 16, 512
QT = T // P
H, DH = 16, 8
E, HID = 8, 512
HC = HID // P
ORDERS = 5
EPS_LN = 1e-5
EPS_DEN = 1e-7
CLIP = float(np.float32(1.0) - np.float32(1e-6))
SCALE = float(np.float32(1.0) / np.sqrt(np.float32(DH)))
GRID = 1.5 * 2.0 ** 19
NEG = -1e30
TERMS8 = [(1, 2), (2, 1), (0, 2), (2, 0), (1, 1), (0, 1), (1, 0), (0, 0)]
TERMS6 = [(0, 2), (2, 0), (1, 1), (0, 1), (1, 0), (0, 0)]
PR = 8
CREDIT = 2
TWO_ONES = float(np.frombuffer(np.uint32(0x3F803F80).tobytes(), np.float32)[0])
GS = 4
TERMS3 = [(1, 0), (0, 1), (0, 0)]
MROW = 96

C_ID, C_WS, C_SUM, C_SEL, C_IO, C_MA, C_MB = 0, 128, 144, 208, 720, 728, 856
C_KEPT, C_N = 728, 984
V_G1, V_B1, V_G2, V_B2, V_BQ, V_BK, V_EB = 0, 1, 2, 3, 4, 5, 6
V_N = V_EB + E * HC
R_BV, R_BP, R_GB = 0, 128, 256
R_N = 264


def beta():
    j = np.arange(6, dtype=np.float32)
    alpha = (j + 1.0) ** (-1.5)
    tail = np.flip(np.cumsum(np.flip(alpha)))
    b = np.concatenate([np.zeros(1, np.float32), tail[1:].astype(np.float32), np.zeros(5, np.float32)])
    return (b / b.sum()).astype(np.float32)


COEF = [float(beta()[p]) * 4.0 ** (p - 1) for p in range(1, ORDERS + 1)]


def constants():
    c = np.zeros((P, C_N), np.float32)
    i = np.arange(P)
    c[i, C_ID + i] = 1
    for h in range(H):
        for p in range(1, 5):
            c[32 * (p - 1) + h, C_WS + h] = COEF[p - 1]
        c[16 + h, C_WS + h] = COEF[4]
        c[DH * h:DH * h + DH, C_SUM + h] = 1
        c[DH * h:DH * h + DH, C_SUM + 32 + 16 + h] = 1
        for t in range(QT):
            c[H * t + h, C_SEL + P * t + DH * h:C_SEL + P * t + DH * h + DH] = 1
    c[:, C_MA:C_MA + P] = np.where(i[None, :] > i[:, None], NEG, 0)
    c[:, C_MB:C_MB + P] = np.where(i[:, None] > i[None, :], NEG, 0)
    c[:, C_IO:C_IO + E] = np.arange(E)
    return c


def block_kernel(nc, x, consts, cols, rows, w_in, w_out, wq, wk, wv, wp, gate_w, ew1, ew2, eb2, out):
    with ExitStack() as ctx:
        place = {}

        def sb(name, shape, dt=F32):
            tensor = ctx.enter_context(nc.sbuf_tensor(name, shape, dt))
            width = int(np.prod(shape[1:])) * (2 if dt == BF16 else 4)
            place[name] = nc.sbuf_base - -(-width // 32) * 32
            return tensor

        def over(name, other, skip, shape):
            return nc.alloc_sbuf_tensor_at(name, shape, F32R, offset=place[other] + skip)

        def sem(name):
            return ctx.enter_context(nc.semaphore(name))

        xs = sb("xs", [P, B * QT, D])
        cst = sb("cst", [P, C_KEPT])
        col = sb("col", [P, V_N])
        row = sb("row", [P, R_N])
        wins = sb("wins", [P, 3, 3 * D], BF16)
        wo_sb = sb("wo_sb", [P, D])
        wq_sb = sb("wq_sb", [P, D])
        wk_sb = sb("wk_sb", [P, D])
        wv_sb = sb("wv_sb", [P, D])
        wp_sb = sb("wp_sb", [P, D])
        gw_sb = sb("gw_sb", [P, E])
        eb2_sb = sb("eb2_sb", [E, D])
        identb = sb("identb", [P, P], BF16)
        maskA = sb("maskA", [P, P], BF16)
        maskB = sb("maskB", [P, P], BF16)
        bqs = sb("bqs", [P, 1])
        one = sb("one", [P, 1])
        negc = sb("negc", [P, 2])
        mhalf = sb("mhalf", [P, QT])

        hn = sb("hn", [P, QT, D])
        hs = sb("hs", [P, QT, D])
        hp = sb("hp", [P, 3, T], BF16)
        F = sb("F", [P, 10, T])
        kv = sb("kv", [P, ORDERS, T])
        va = sb("va", [P, T])
        ksum = sb("ksum", [P, T])
        den = sb("den", [P, QT * H])
        rdT = sb("rdT", [QT * H, P])
        qf = sb("qf", [P, T])
        kf = sb("kf", [P, T])
        lnT = sb("lnT", [P, T])
        qs = sb("qs", [P, 3, T], BF16)
        ks = sb("ks", [P, 3, T], BF16)
        nm = sb("nm", [P, H, QT])
        nms = sb("nms", [QT * H, 3, P], BF16)
        nmr = sb("nmr", [QT * H, P])
        stack = sb("stack", [P, 2, 2, H, T], BF16)
        qst = [stack[:, i, 0, :, :] for i in range(2)]
        kst = [stack[:, i, 1, :, :] for i in range(2)]
        vb = sb("vb", [P, 2, QT, D])
        hk = sb("hk", [P, 2, QT, D])
        vaug = sb("vaug", [P, QT, H, 32])
        x2t = sb("x2t", [P, QT, D])
        hb = sb("hb", [P, QT, D])
        pr = sb("pr", [P, PR, T])
        oT = sb("oT", [P, 2, T])
        yt = sb("yt", [P, QT, D])
        rec = sb("rec", [P, QT, 4])
        lg = sb("lg", [P, QT, E])
        top = sb("top", [P, QT, 8])
        topi = sb("topi", [P, QT, 8], U32)
        topf = sb("topf", [P, QT, 8])
        gt = sb("gt", [P, 4, QT])
        gd = sb("gd", [P, QT])
        oh = sb("oh", [P, 2, QT, E])
        wf = sb("wf", [P, QT, E])
        wd = nc.dram_tensor("wd", (B, E, T), F32, kind="Internal").ap()
        h2d = nc.dram_tensor("h2d", (B, P, T), F32, kind="Internal").ap()
        norm = {}
        for c in "amb":
            norm[c] = dict(st=sb("st" + c, [P, QT, 6]), mv=sb("mv" + c, [P, QT, 2]), lnv=sb("lnv" + c, [P, 4, QT]),
                           rstd=sb("rstd" + c, [P, QT]),
                           stats=sem("ln_stats_" + c), var=sem("ln_var_" + c), step=sem("ln_step_" + c),
                           ready=sem("ln_rstd_" + c), out=sem("ln_out_" + c))
        w1_sb = qst[0].rearrange("p h n -> p (h n)").bitcast(F32).rearrange("p (e n) -> p e n", e=E)
        w2_sb = kst[0].rearrange("p h n -> p (h n)").bitcast(F32).rearrange("p (c n) -> p c n", n=D)
        half = 2 * H * T * 2
        w1p = [over("w1_first", "stack", half, [P, E, HID]), over("w1_second", "stack", 0, [P, E, HID])]
        w2p = [over("w2_first", "stack", half + half // 2, [P, E * HC, D]), over("w2_second", "stack", half // 2, [P, E * HC, D])]
        h2r = pr[:, 0:2, :]
        h2p = [over("h2_first", "pr", 4 * T * 2, [P, 2, T]), over("h2_second", "pr", 4 * T * 4, [P, 2, T])]
        hid_first = over("hid_first", "F", 0, [P, 2 * HC, T])
        hid_second = [over("hid_second", "kv", 0, [P, ORDERS, T]), over("hid_second_rest", "vaug", 0, [P, 2 * HC - ORDERS, T])]
        hidh = [hid_first[:, i, :] for i in range(2 * HC)]
        hidl = [hid_second[i // ORDERS][:, i % ORDERS, :] for i in range(2 * HC)]
        wB = [t[:, i, :, :].rearrange("p t d -> p (t d)") for t in (vb, hk) for i in range(2)]
        acc = [ksum[:, :], yt[:, :, :].rearrange("p t d -> p (t d)")]
        term = [va[:, :], lnT[:, :]]
        gel = [pr[:, 6, :], pr[:, 7, :], oT[:, 0, :], oT[:, 1, :]]

        qx, kx = [F[:, i, :] for i in range(5)], [F[:, 5 + i, :] for i in range(5)]
        hr = F[:, 9, :]
        y = yt[:, :, :].rearrange("p t (h d) -> p t h d", h=H)
        win = kv[:, 0:3 * D // T + 1, :].rearrange("p a n -> p (a n)")[:, 0:3 * D]
        masks = kv[:, 4, 0:C_N - C_KEPT]
        ha = hn
        outT = va
        yT = hn[:, :, :].rearrange("p t d -> p (t d)")
        h2 = lnT
        wfT = h2[0:E, :].rearrange("e (t n) -> e t n", t=QT)
        ident = cst[:, C_ID:C_ID + P]

        X, Y, Z, V = (ctx.enter_context(nc.psum_tensor(n, [P, T], F32)) for n in ("front0", "front1", "back0", "back1"))
        ringE = [ctx.enter_context(nc.psum_tensor(f"scores{i}", [P, T], F32)) for i in range(2)]
        ringM = [ctx.enter_context(nc.psum_tensor(f"maxima{i}", [P, T], F32)) for i in range(2)]

        names = """
            stack_set w_loaded x_loaded e_loaded w_split const_ready pool_const tr0 h_grid h_rest h_mid
            h_split hq_mm hk_mm hv_mm hk_ev hq_ev hv_ev k_clip q_clip k_sq q_sq k_t35 q_t35 k_t24 q_t24
            ks_mm qs_mm k_scan d_prod den_mm den_eps den_rec rdT_mm rdT_ev rdB_mm kv_ready kv_sum qk_prod
            n_add outT_ready o1_mm x1_ready tr1 lnT_ready aq_mm ak_mm av_mm qf_ready kf_ready v_ev
            p1_ready r1_ready p2_ready p3_ready v_ready stack_dma smax_mm smax_red nmT_mm n1_ready
            nr_ready n2_ready n3_ready max_dma h_kept sc_mm exp_ready pr_used pv_ev ot_tr rec_ready
            y_ready yT_mm yT_ev o2_mm x2_ready xsum tr3 h2_ready h2_kept gate_mm lg_ready top_ready
            topi_ready topf_ready g_step g_exp oh_ready wf_ready wfT_mm wfT_ev b2_mm xb_ready w_kept
            h2_loaded wh_ready wl_ready h2_hi h2_lo y_scaled fin_mm out_ready mid_mm mid_ready hid_hi
            hid_lo y2_mm acc_ready stored""".split()
        W = type("Sems", (), {n: sem(n) for n in names})
        wb_loaded = [sem(f"wb_loaded{i}") for i in range(4)]
        TILES = 3 * H
        STEPS = TILES // 4
        KEYS = ((0,), (1,), (2, 3))
        MAXIMA = [(g + h, n, t) for g in range(0, H, 4) for t, n in ((0, 4), (1, 2), (2, 1), (3, 1)) for h in range(0, 4, n)]
        NMAX = len(MAXIMA)
        SLOTS = 60
        SPLIT_AT = (3, 5, 10, 12, 22, 25, 35, 36)
        MAX_AT = {k: [3 * (k // 4) + k % 4 - 1] for k in range(TILES) if k % 4}
        MAX_AT.update({TILES + i: [3 * STEPS + 2 * i, 3 * STEPS + 2 * i + 1] for i in range((NMAX - 3 * STEPS) // 2)})

        def wait_apart(engine, semaphore, value):
            engine.wait_ge(semaphore, value)
            engine.nop(nofuse=True)

        def pipelined(engine, body):
            def edge(t):
                stages = [t + i if 0 <= t + i < B else None for i in range(5)]
                body(*stages, (t + 1) % 2)
            for t in range(-4, 0):
                edge(t)
            with engine.Fori(0, (B - 4) // 2) as pair:
                t = pair * 2
                body(t, t + 1, t + 2, t + 3, t + 4, 1)
                body(t + 1, t + 2, t + 3, t + 4, t + 5, 0)
            for t in range(B - 4, B):
                edge(t)

        def batches(engine, body):
            body(0, 0, False, True)
            with engine.Fori(0, B // 2 - 1) as pair:
                body(pair * 2 + 1, 1, True, True)
                body(pair * 2 + 2, 0, True, True)
            body(B - 1, 1, True, False)

        block = ctx.enter_context(nc.Block())

        @block.sync
        def _(sp):
            loads = [(cst, consts[:, 0:C_KEPT]), (masks, consts[:, C_KEPT:C_N]), (col, cols), (row, rows), (win, w_in),
                     (wo_sb, w_out), (wq_sb, wq), (wk_sb, wk), (wv_sb, wv), (wp_sb, wp), (gw_sb, gate_w), (eb2_sb, eb2)]
            xv = x.rearrange("b (t p) d -> b p t d", p=P)

            def load_x(b):
                sp.dma_start(xs[:, bass.ds(b * QT, QT), :],
                             xv[bass.ds(b, 1), :, :, :].rearrange("a p t d -> (a p) t d")).then_inc(W.x_loaded, 16)

            load_x(0)
            for dst, src in loads:
                sp.dma_start(dst if dst is masks or dst is win else dst[:, :], src).then_inc(W.w_loaded, 16)
            sp.wait_ge(W.x_loaded, 16)
            with sp.Fori(1, B) as b:
                load_x(b)
                wait_apart(sp, W.x_loaded, b * 16 + 16)
            ov = out.rearrange("b (t p) d -> b p t d", p=P)

            def load(b, p):
                sp.dma_start(h2r[:, p, :], h2d[bass.ds(b, 1), :, :].rearrange("a p n -> (a p) n")).then_inc(W.h2_loaded, 16)

            def load_weights(b, e):
                if not (isinstance(b, int) and b == 0 and e < 4):
                    sp.wait_ge(W.y_scaled, b * E + e - 3 + CREDIT)
                sp.dma_start(wB[e % 4], wd[bass.ds(b, 1), e:e + 1, :].rearrange("a e n -> (a e) n").broadcast_to((P, T))).then_inc(wb_loaded[e % 4], 16)

            def store(b):
                sp.wait_ge(W.out_ready, b + 1)
                sp.dma_start(ov[bass.ds(b, 1), :, :, :].rearrange("a p t d -> (a p) t d"), xs[:, bass.ds(b * QT, QT), :]).then_inc(W.stored, 16)

            def body(t, b, m, g, f, p):
                if b is None and t is not None:
                    sp.wait_ge(W.pr_used, B * STEPS)
                    sp.wait_ge(W.h2_kept, 16 * (B - 1))
                    load(0, 0)
                if t is not None:
                    sp.wait_ge(W.h2_ready, t + 1)
                    sp.dma_start(h2d[bass.ds(t, 1), :, :].rearrange("a p n -> (a p) n"), h2[:, :]).then_inc(W.h2_kept, 16)
                    sp.wait_ge(W.wfT_ev, t + 1)
                    sp.dma_start(wd[bass.ds(t, 1), :, :].rearrange("a e n -> (a e) n"), wfT.rearrange("e t n -> e (t n)")).then_inc(W.w_kept, 16)
                if g is not None:
                    sp.wait_ge(W.p2_ready, g * 2 + 2)
                    sp.wait_ge(W.p3_ready, g * 2 + 2)
                    if isinstance(g, int) and g == 0:
                        sp.wait_ge(W.stack_set, 4)
                    if b is not None:
                        sp.wait_ge(W.sc_mm, b * TILES + TILES)
                    for n, (i, j) in enumerate(TERMS6):
                        sp.dma_start(qst[p][DH * n:DH * n + DH, :, :], qs[:, i, :]).then_inc(W.stack_dma, 16)
                        sp.dma_start(kst[p][DH * n:DH * n + DH, :, :], ks[:, j, :]).then_inc(W.stack_dma, 16)
                if m is not None:
                    sp.wait_ge(W.n2_ready, m + 1)
                    sp.wait_ge(W.n3_ready, m + 1)
                    for i in range(3):
                        sp.dma_start(qst[1 - p][MROW + i:MROW + i + 1, :, :], nms[:, i, :]).then_inc(W.max_dma, 16)
                if isinstance(b, int) and b == B - 2:
                    sp.wait_ge(W.sc_mm, (B - 1) * TILES)
                    sp.dma_start(w1_sb, ew1.rearrange("e d n -> d e n")).then_inc(W.e_loaded, 16)
                    for e in range(E):
                        sp.dma_start(w2_sb[:, e * HC:(e + 1) * HC, :], ew2[e].rearrange("(c p) d -> p c d", p=P)).then_inc(W.e_loaded, 16)

            pipelined(sp, body)
            sp.wait_ge(W.h2_kept, 16 * B)
            sp.wait_ge(W.w_kept, 16 * B)

            def experts(b, p, before, after):
                if after:
                    if before:
                        sp.wait_ge(W.h2_lo, b)
                    sp.wait_ge(W.h2_loaded, b * 16 + 16)
                    load(b + 1, 1 - p)
                for e in range(4):
                    load_weights(b, e)
                if before:
                    store(b - 1)
                for e in range(4, E):
                    load_weights(b, e)

            batches(sp, experts)
            store(B - 1)
            sp.wait_ge(W.stored, 16 * B)

        def ln_stats(c, n, src):
            k = norm[c]
            for t in range(QT):
                nc.vector.bn_stats(k["st"][:, t, :], src(t)).then_inc(k["stats"], 1)
            wait_apart(nc.vector, k["stats"], n * QT + QT)
            for t in range(QT):
                nc.vector.bn_aggr(k["mv"][:, t, :], k["st"][:, t, :]).then_inc(k["var"], 1)

        def ln_rsqrt(c, n):
            g, k = nc.gpsimd, norm[c]
            ve, y0, a, b_ = (k["lnv"][:, i, :] for i in range(4))
            steps = [
                lambda: g.tensor_scalar(ve, k["mv"][:, :, 1], EPS_LN, None, ALU.add),
                lambda: g.tensor_tensor(y0, ve, mhalf[:, :], ALU.pow),
                lambda: g.tensor_tensor(a, y0, y0, ALU.mult),
                lambda: g.tensor_tensor(b_, a, ve, ALU.mult),
                lambda: g.tensor_scalar(a, b_, -0.5, 1.5, ALU.mult, ALU.add),
            ]
            wait_apart(g, k["var"], n * QT + QT)
            for i, step in enumerate(steps):
                step().then_inc(k["step"], 1)
                wait_apart(g, k["step"], n * len(steps) + i + 1)
            g.tensor_tensor(k["rstd"][:, :], y0, a, ALU.mult).then_inc(k["ready"], 1)

        def ln_apply(c, n, src, dst):
            k = norm[c]
            nc.vector.wait_ge(k["ready"], n + 1)
            for t in range(QT):
                nc.vector.tensor_scalar(dst(t), src(t), k["mv"][:, t, 0:1], k["rstd"][:, t:t + 1],
                                        ALU.subtract, ALU.mult).then_inc(k["out"], 1)

        @block.vector
        def _(dve):
            v = nc.vector
            v.memset(one[:, :], 1.0)
            v.memset(negc[:, 0:1], -0.5)
            v.memset(negc[:, 1:2], -0.625).then_inc(W.const_ready, 1)
            v.memset(vaug[:, :, :, :], 0.0).then_inc(W.const_ready, 1)
            dve.wait_ge(W.const_ready, 2)
            v.memset(vaug[:, :, :, DH:DH + 1], 1.0).then_inc(W.const_ready, 1)
            dve.wait_ge(W.w_loaded, 16 * 12)
            v.tensor_copy(identb[:, :], ident)
            v.tensor_copy(maskA[:, :], masks[:, 0:P])
            v.tensor_copy(maskB[:, :], masks[:, P:2 * P])
            v.tensor_scalar(bqs[:, :], col[:, V_BQ:V_BQ + 1], SCALE, None, ALU.mult).then_inc(W.const_ready, 1)
            v.tensor_copy(wins[:, 0, :], win).then_inc(W.w_split, 1)
            dve.wait_ge(W.w_split, 1)
            v.tensor_tensor(win, win, wins[:, 0, :], ALU.subtract).then_inc(W.w_split, 1)
            dve.wait_ge(W.w_split, 2)
            v.tensor_copy(wins[:, 1, :], win).then_inc(W.w_split, 1)
            dve.wait_ge(W.w_split, 3)
            v.tensor_tensor(wins[:, 2, :], win, wins[:, 1, :], ALU.subtract).then_inc(W.w_split, 1)

            def tile_of(b):
                return lambda t: xs[:, bass.ds(b * QT + t, 1), :].rearrange("p a d -> p (a d)")

            def batch_of(b):
                return xs[:, bass.ds(b * QT, QT), :]

            four = lambda a: a.rearrange("p (t d) -> p t d", t=QT)

            def stats0(f):
                wait_apart(dve, W.x_loaded, f * 16 + 16)
                ln_stats("a", f, tile_of(f))

            def apply0(f):
                ln_apply("a", f, tile_of(f), lambda t: hn[:, t, :])

            def split_h(f):
                dve.wait_ge(W.tr0, f + 1)
                v.tensor_scalar(hp[:, 0, :], X[:, :], GRID, GRID, ALU.add, ALU.subtract).then_inc(W.h_grid, 1)

            def split_h2(f):
                dve.wait_ge(W.h_grid, f + 1)
                v.tensor_tensor(hr, X[:, :], hp[:, 0, :], ALU.subtract).then_inc(W.h_rest, 1)

            def split_h3(f):
                dve.wait_ge(W.h_mid, f + 1)
                v.tensor_tensor(hp[:, 2, :], hr, hp[:, 1, :], ALU.subtract).then_inc(W.h_split, 1)

            def clip(f, z, evac, done):
                dve.wait_ge(evac, f + 1)
                v.tensor_scalar(z[0], z[0], -CLIP, CLIP, ALU.max, ALU.min).then_inc(done, 1)

            def third_order(f, z, sq, done):
                dve.wait_ge(sq, f * 3 + 3)
                v.scalar_tensor_tensor(z[2], z[1], -0.75, z[0], ALU.add, ALU.mult).then_inc(done, 1)

            def fifth_order(f, z, sq, done):
                v.scalar_tensor_tensor(z[4], z[4], -5 / 64, z[0], ALU.add, ALU.mult).then_inc(done, 1)

            def times_v(f, orders):
                dve.wait_ge(W.hv_ev, f + 1)
                dve.wait_ge(W.k_t24, f * 2 + 2)
                dve.wait_ge(W.k_t35, f * 2 + 2)
                for p in orders:
                    v.scalar_tensor_tensor(kv[:, p, :], kx[p], COEF[p], va[:, :], ALU.mult, ALU.mult).then_inc(W.kv_ready, 1)

            def running(out_, in_, done):
                v.tensor_tensor_scan(out_, one[:, 0:1].to_broadcast((P, T)), in_, 0.0, ALU.mult, ALU.add).then_inc(done, 1)

            def sum_k(f):
                dve.wait_ge(W.ks_mm, f + 1)
                running(ksum[:, :], X[:, :], W.k_scan)

            def den_terms(f):
                dve.wait_ge(W.qs_mm, f + 1)
                dve.wait_ge(W.k_scan, f + 1)
                v.tensor_tensor(ksum[:, :], Y[:, :], ksum[:, :], ALU.mult).then_inc(W.d_prod, 1)

            def sum_kv(f, orders):
                for p in orders:
                    dve.wait_ge(W.kv_ready, f * ORDERS + p + 1)
                    running(kv[:, p, :], kv[:, p, :], W.kv_sum)

            def invert_den(f):
                dve.wait_ge(W.den_mm, f + 1)
                v.tensor_scalar(den[:, :], X[:, 0:QT * H], EPS_DEN, None, ALU.add).then_inc(W.den_eps, 1)
                dve.wait_ge(W.den_eps, f + 1)
                v.reciprocal(den[:, :], den[:, :]).then_inc(W.den_rec, 1)

            def ratio(f):
                dve.wait_ge(W.n_add, f * 4 + 4)
                dve.wait_ge(W.rdB_mm, f + 1)
                v.tensor_tensor(outT[:, :], Y[:, :], kv[:, 1, :], ALU.mult).then_inc(W.outT_ready, 1)

            def add_x1(f):
                dve.wait_ge(W.o1_mm, f + 1)
                v.tensor_tensor(batch_of(f), four(X[:, :]), batch_of(f), ALU.add).then_inc(W.x1_ready, 1)
                wait_apart(dve, W.x1_ready, f + 1)

            def stats1(m):
                ln_stats("m", m * 2, tile_of(m))

            def apply1(m):
                if not isinstance(m, int) or m:
                    dve.wait_ge(W.h_kept, m)
                ln_apply("m", m * 2, tile_of(m), lambda t: hs[:, t, :])
                wait_apart(dve, norm["m"]["out"], m * 8 + 4)

            def stats2(m):
                ln_stats("m", m * 2 + 1, lambda t: hs[:, t, :])

            def apply2(m):
                ln_apply("m", m * 2 + 1, lambda t: hs[:, t, :], lambda t: ha[:, t, :])

            def third_part(m, n, whole, parts):
                dve.wait_ge(W.p2_ready, m * 2 + n)
                v.tensor_tensor(parts[:, 2, :], whole[:, :], parts[:, 1, :], ALU.subtract).then_inc(W.p3_ready, 1)

            def maximum(m, n):
                h, heads, t = MAXIMA[n]
                dve.wait_ge(W.smax_mm, m * NMAX + n + 1)
                v.tensor_reduce(nm[:, h:h + heads, t], ringM[n % 2][:, 0:heads * (t + 1) * P].rearrange("p (h n) -> p h n", h=heads),
                                AX.X, ALU.max, negate=True).then_inc(W.smax_red, 1)

            def max_rest(m, step):
                if step == 0:
                    dve.wait_ge(W.n1_ready, m + 1)
                    v.tensor_tensor(nmr[:, :], V[0:QT * H, 0:P], nms[:, 0, :], ALU.subtract).then_inc(W.nr_ready, 1)
                else:
                    dve.wait_ge(W.n2_ready, m + 1)
                    v.tensor_tensor(nms[:, 2, :], nmr[:, :], nms[:, 1, :], ALU.subtract).then_inc(W.n3_ready, 1)

            def add_bv(b, p):
                dve.wait_ge(W.v_ev, b + 1)
                if not isinstance(b, int) or b:
                    dve.wait_ge(W.pr_used, b * STEPS)
                for t in range(QT):
                    v.tensor_tensor(vaug[:, t, :, 0:DH], vb[:, p, t, :].rearrange("p (h d) -> p h d", h=H),
                                    row[:, R_BV:R_BV + D].rearrange("p (h d) -> p h d", h=H), ALU.add).then_inc(W.v_ready, 1)

            def normalise(b, g):
                dve.wait_ge(W.ot_tr, b * 4 + g + 1)
                o4 = Z[:, :].rearrange("p (t j c) -> p t j c", t=QT, j=4)
                v.reciprocal(rec[:, :, :], o4[:, :, :, DH]).then_inc(W.rec_ready, 1)
                dve.wait_ge(W.rec_ready, b * 4 + g + 1)
                for t in range(QT):
                    v.tensor_tensor(y[:, t, 4 * g:4 * g + 4, :], o4[:, t, :, 0:DH],
                                    rec[:, t, :].unsqueeze(2).to_broadcast((P, 4, DH)), ALU.mult).then_inc(W.y_ready, 1)

            def x2(b, p):
                dve.wait_ge(W.o2_mm, b + 1)
                dve.wait_ge(W.h_kept, b + 1)
                if not isinstance(b, int) or b:
                    dve.wait_ge(W.xsum, b)
                v.tensor_tensor(x2t[:, :, :], four(V[:, :]), hk[:, p, :, :], ALU.add).then_inc(W.x2_ready, 1)

            def stats3(b):
                wait_apart(dve, W.x2_ready, b + 1)
                ln_stats("b", b, lambda t: x2t[:, t, :])

            def apply3(b):
                ln_apply("b", b, lambda t: x2t[:, t, :], lambda t: hb[:, t, :])

            def gate_top(b):
                dve.wait_ge(W.gate_mm, b + 1)
                v.tensor_tensor(lg[:, :, :], Z[:, 0:QT * E].rearrange("p (t e) -> p t e", t=QT),
                                row[:, R_GB:R_GB + E].unsqueeze(1).to_broadcast((P, QT, E)), ALU.add).then_inc(W.lg_ready, 1)
                wait_apart(dve, W.lg_ready, b + 1)
                for t in range(QT):
                    v.max(top[:, t, :], lg[:, t, :]).then_inc(W.top_ready, 1)
                wait_apart(dve, W.top_ready, b * QT + QT)
                v.tensor_tensor(gt[:, 0, :], top[:, :, 1], top[:, :, 0], ALU.subtract).then_inc(W.g_step, 1)
                for t in range(QT):
                    v.max_index(topi[:, t, :], top[:, t, :], lg[:, t, :]).then_inc(W.topi_ready, 1)
                dve.wait_ge(W.topi_ready, b * QT + QT)
                v.tensor_copy(topf[:, :, :], topi[:, :, :]).then_inc(W.topf_ready, 1)

            def gate_weights(b):
                dve.wait_ge(W.g_exp, b + 1)
                v.tensor_scalar(gd[:, :], gt[:, 1, :], 1.0, None, ALU.add).then_inc(W.g_step, 1)
                dve.wait_ge(W.g_step, b * 4 + 2)
                v.reciprocal(gt[:, 2, :], gd[:, :]).then_inc(W.g_step, 1)
                dve.wait_ge(W.g_step, b * 4 + 3)
                v.tensor_tensor(gt[:, 3, :], gt[:, 1, :], gt[:, 2, :], ALU.mult).then_inc(W.g_step, 1)
                dve.wait_ge(W.topf_ready, b + 1)
                dve.wait_ge(W.g_step, b * 4 + 4)
                for i in range(2):
                    v.tensor_tensor(oh[:, i, :, :], cst[:, C_IO:C_IO + E].unsqueeze(1).to_broadcast((P, QT, E)),
                                    topf[:, :, i:i + 1].to_broadcast((P, QT, E)), ALU.is_equal).then_inc(W.oh_ready, 1)
                dve.wait_ge(W.oh_ready, b * 4 + 2)
                for i in range(2):
                    v.tensor_tensor(oh[:, i, :, :], oh[:, i, :, :], gt[:, 2 + i, :].unsqueeze(2).to_broadcast((P, QT, E)),
                                    ALU.mult).then_inc(W.oh_ready, 1)
                dve.wait_ge(W.oh_ready, b * 4 + 4)
                v.tensor_tensor(wf[:, :, :], oh[:, 0, :, :], oh[:, 1, :, :], ALU.add).then_inc(W.wf_ready, 1)

            def add_b2(b):
                dve.wait_ge(W.b2_mm, b + 1)
                dve.wait_ge(W.xsum, b + 1)
                v.tensor_tensor(batch_of(b), four(Z[:, :]), batch_of(b), ALU.add).then_inc(W.xb_ready, 1)

            def second(b, p, whole, parts, first, done):
                dve.wait_ge(first, b + 1)
                v.tensor_tensor(parts[1], whole, parts[0], ALU.subtract).then_inc(done, 1)

            def second_h2(b, p):
                second(b, p, h2r[:, p, :], [h2p[i][:, p, :] for i in range(2)], W.h2_hi, W.h2_lo)

            def second_weights(e):
                dve.wait_ge(W.wh_ready, 2 * e + 1)
                v.tensor_tensor(w1p[1][:, e, :], w1_sb[:, e, :], w1p[0][:, e, :], ALU.subtract).then_inc(W.wl_ready, 1)
                dve.wait_ge(W.wh_ready, 2 * e + 2)
                v.tensor_tensor(w2p[1][:, e * HC:(e + 1) * HC, :], w2_sb[:, e * HC:(e + 1) * HC, :],
                                w2p[0][:, e * HC:(e + 1) * HC, :], ALU.subtract).then_inc(W.wl_ready, 1)
                if e == 0:
                    second_h2(0, 0)
            def body(t, b, m, g, f, p):
                for n in range(SLOTS):
                    if b is None and t is not None:
                        if n in SPLIT_AT:
                            second_weights(SPLIT_AT.index(n))
                    at = lambda place, stage: n == place and stage is not None
                    if m is not None:
                        for i in MAX_AT.get(n, ()):
                            maximum(m, i)
                    if at(0, b):
                        add_bv(b, p)
                    if at(0, g):
                        stats1(g)
                    if at(0, t):
                        stats3(t)
                    if at(1, f):
                        stats0(f)
                    if at(4, g):
                        apply1(g)
                    if at(6, f):
                        apply0(f)
                    if at(8, g):
                        stats2(g)
                    if at(10, t):
                        apply3(t)
                    if at(10, f):
                        split_h(f)
                    if at(11, f):
                        split_h2(f)
                    if at(13, g):
                        apply2(g)
                    if at(15, f):
                        split_h3(f)
                    if at(20, t):
                        gate_top(t)
                    if at(23, b):
                        normalise(b, 0)
                    if at(23, f):
                        clip(f, kx, W.hk_ev, W.k_clip)
                    if at(25, t):
                        gate_weights(t)
                    if at(26, f):
                        clip(f, qx, W.hq_ev, W.q_clip)
                    if at(29, f):
                        third_order(f, kx, W.k_sq, W.k_t35)
                    if at(31, f):
                        fifth_order(f, kx, W.k_sq, W.k_t35)
                    if at(33, t):
                        add_b2(t)
                    if at(34, f):
                        third_order(f, qx, W.q_sq, W.q_t35)
                    if at(34, f):
                        fifth_order(f, qx, W.q_sq, W.q_t35)
                    if at(35, f):
                        times_v(f, (0, 1))
                    if at(35, f):
                        times_v(f, (2,))
                    if at(35, f):
                        times_v(f, (3, 4))
                    if at(37, b):
                        normalise(b, 1)
                    if at(37, f):
                        sum_kv(f, (0,))
                    if at(38, f):
                        sum_kv(f, (1,))
                    if at(39, f):
                        sum_kv(f, (2,))
                    if at(40, f):
                        sum_kv(f, (3, 4))
                    if at(41, f):
                        sum_k(f)
                    if at(43, b):
                        normalise(b, 2)
                    if at(44, f):
                        den_terms(f)
                    if at(46, g):
                        third_part(g, 2, kf, ks)
                    if at(47, g):
                        third_part(g, 1, qf, qs)
                    if at(48, f):
                        invert_den(f)
                    if at(51, b):
                        normalise(b, 3)
                    if at(54, m):
                        max_rest(m, 0)
                    if at(55, m):
                        max_rest(m, 1)
                    if at(56, f):
                        ratio(f)
                    if at(56, b):
                        x2(b, p)
                    if at(59, f):
                        add_x1(f)

            pipelined(dve, body)

            dve.wait_ge(W.xb_ready, B)
            dve.sem_inc(W.y_scaled, CREDIT)
            dve.sem_inc(W.hid_lo, GS)

            def accumulate(b, p, e):
                dve.wait_ge(W.y2_mm, b * E + e + 1 + CREDIT)
                dve.wait_ge(wb_loaded[e % 4], b * 32 + 16 * (e // 4) + 16)
                v.tensor_tensor(term[e % 2] if e else acc[p], (Z, V)[e % 2][:, :], wB[e % 4], ALU.mult).then_inc(W.y_scaled, 1)
                if e:
                    dve.wait_ge(W.y_scaled, b * E + e + 1 + CREDIT)
                    if e > 1:
                        dve.wait_ge(W.acc_ready, b * (E - 1) + e - 1)
                    v.tensor_tensor(acc[p], acc[p], term[e % 2], ALU.add).then_inc(W.acc_ready, 1)

            def add_experts(b, p):
                dve.wait_ge(W.fin_mm, b + 1)
                v.tensor_tensor(batch_of(b), four(ringM[p][:, :]), batch_of(b), ALU.add).then_inc(W.out_ready, 1)

            def experts(b, p, before, after):
                for e in range(E):
                    for c in range(HC):
                        n = e * HC + c
                        dve.wait_ge(W.hid_hi, b * (E * HC) + n + 1)
                        v.tensor_tensor(hidl[e % 2 * HC + c], gel[n % GS], hidh[e % 2 * HC + c], ALU.subtract).then_inc(W.hid_lo, 1)
                    if e == 4 and after:
                        second_h2(b + 1, 1 - p)
                    if e == 0 and before:
                        accumulate(b - 1, 1 - p, E - 1)
                    if e == 2 and before:
                        add_experts(b - 1, 1 - p)
                    if e:
                        accumulate(b, p, e - 1)

            batches(dve, experts)
            accumulate(B - 1, 1, E - 1)
            add_experts(B - 1, 1)

        @block.scalar
        def _(act):
            a = nc.scalar
            act.wait_ge(W.const_ready, 4)
            act.wait_ge(W.w_loaded, 16 * 12)

            def second_part(f):
                act.wait_ge(W.h_rest, f + 1)
                a.activation(hp[:, 1, :], hr, ACT.Copy).then_inc(W.h_mid, 1)

            def take_k(f):
                act.wait_ge(W.hk_mm, f + 1)
                a.activation(kx[0], Y[:, :], ACT.Copy, scale=SCALE).then_inc(W.hk_ev, 1)

            def take_q(f):
                act.wait_ge(W.hq_mm, f + 1)
                a.activation(qx[0], X[:, :], ACT.Copy, scale=SCALE).then_inc(W.hq_ev, 1)

            def take_v(f):
                act.wait_ge(W.hv_mm, f + 1)
                a.activation(va[:, :], Y[:, :], ACT.Copy).then_inc(W.hv_ev, 1)

            def square(f, z, clipped, sq):
                act.wait_ge(clipped, f + 1)
                a.activation(z[1], z[0], ACT.Square).then_inc(sq, 1)

            def square2(f, z, sq):
                act.wait_ge(sq, f * 3 + 1)
                a.activation(z[3], z[1], ACT.Square, bias=negc[:, 0:1]).then_inc(sq, 1)

            def square3(f, z, sq):
                a.activation(z[4], z[1], ACT.Square, bias=negc[:, 1:2]).then_inc(sq, 1)

            def take_rden(f):
                act.wait_ge(W.rdT_mm, f + 1)
                a.activation(rdT[:, :], X[0:QT * H, P:2 * P], ACT.Copy).then_inc(W.rdT_ev, 1)

            def affine1(m, t):
                act.wait_ge(W.tr1, m + 1)
                if t is not None:
                    act.wait_ge(W.b2_mm, t + 1)
                a.activation(lnT[:, :], Y[:, :], ACT.Identity, bias=col[:, V_B1:V_B1 + 1],
                             scale=col[:, V_G1:V_G1 + 1]).then_inc(W.lnT_ready, 1)

            def take_qk(m, step):
                if step == 0:
                    act.wait_ge(W.aq_mm, m + 1)
                    a.activation(qf[:, :], X[:, :], ACT.Identity, bias=bqs[:, :], scale=SCALE).then_inc(W.qf_ready, 1)
                if step == 1:
                    act.wait_ge(W.ak_mm, m + 1)
                    a.activation(kf[:, :], Y[:, :], ACT.Identity, bias=col[:, V_BK:V_BK + 1]).then_inc(W.kf_ready, 1)
                if step == 2:
                    if not isinstance(m, int) or m:
                        act.wait_ge(W.stack_dma, m * (16 * 12))
                    act.wait_ge(W.qf_ready, m + 1)
                    a.activation(qs[:, 0, :], qf[:, :], ACT.Copy).then_inc(W.p1_ready, 1)
                    act.wait_ge(W.kf_ready, m + 1)
                    a.activation(ks[:, 0, :], kf[:, :], ACT.Copy).then_inc(W.p1_ready, 1)

            def take_v2(m, b, p):
                act.wait_ge(W.av_mm, m + 1)
                if b is not None:
                    act.wait_ge(W.v_ready, b * QT + QT)
                a.activation(vb[:, p, :, :], X[:, :].rearrange("p (t d) -> p t d", t=QT), ACT.Copy).then_inc(W.v_ev, 1)

            def second_parts(m, n, rest, parts):
                act.wait_ge(W.r1_ready, m * 2 + n)
                a.activation(parts[:, 1, :], rest[:, :], ACT.Copy).then_inc(W.p2_ready, 1)

            def max_parts(f, step):
                if step == 0:
                    act.wait_ge(W.nmT_mm, f + 1)
                    a.activation(nms[:, 0, :], V[0:QT * H, 0:P], ACT.Copy).then_inc(W.n1_ready, 1)
                else:
                    act.wait_ge(W.nr_ready, f + 1)
                    a.activation(nms[:, 1, :], nmr[:, :], ACT.Copy).then_inc(W.n2_ready, 1)

            def exps(b, n):
                width = T if (n // 4) % 3 == 0 else T - P
                act.wait_ge(W.sc_mm, b * TILES + n + 1)
                if n >= PR:
                    act.wait_ge(W.pr_used, b * STEPS + (n - PR) // 4 + 1)
                a.activation(pr[:, n % PR, 0:width], ringE[n % 2][:, 0:width], ACT.Exp).then_inc(W.exp_ready, 1)

            def evacuate(b, g):
                act.wait_ge(W.pr_used, b * STEPS + 3 * (g + 1))
                a.activation(oT[:, g % 2, :], V[:, :], ACT.Copy).then_inc(W.pv_ev, 1)

            def take_y(b):
                act.wait_ge(W.yT_mm, b + 1)
                a.activation(yT[:, :], Z[:, :], ACT.Copy).then_inc(W.yT_ev, 1)

            def affine2(b):
                act.wait_ge(W.tr3, b + 1)
                a.activation(h2[:, :], Z[:, :], ACT.Identity, bias=col[:, V_B2:V_B2 + 1],
                             scale=col[:, V_G2:V_G2 + 1]).then_inc(W.h2_ready, 1)

            def gate_exp(b):
                act.wait_ge(W.g_step, b * 4 + 1)
                a.activation(gt[:, 1, :], gt[:, 0, :], ACT.Exp).then_inc(W.g_exp, 1)

            def take_weights(b):
                act.wait_ge(W.wfT_mm, b + 1)
                act.wait_ge(W.h2_kept, b * 16 + 16)
                a.activation(wfT[:, :, :], Z[0:E, :].rearrange("p (t n) -> p t n", t=QT), ACT.Copy).then_inc(W.wfT_ev, 1)

            def first_weights(e):
                if e == 0:
                    act.wait_ge(W.e_loaded, 16 * (1 + E))
                    act.wait_ge(W.sc_mm, B * TILES)
                a.activation(w1p[0][:, e, :], w1_sb[:, e, :], ACT.Copy).then_inc(W.wh_ready, 1)
                a.activation(w2p[0][:, e * HC:(e + 1) * HC, :], w2_sb[:, e * HC:(e + 1) * HC, :], ACT.Copy).then_inc(W.wh_ready, 1)
                if e == 0:
                    act.wait_ge(W.h2_loaded, 16)
                    a.activation(h2p[0][:, 0, :], h2r[:, 0, :], ACT.Copy).then_inc(W.h2_hi, 1)

            def body(t, b, m, g, f, p):
                for n in range(SLOTS):
                    if b is None and t is not None and n in SPLIT_AT:
                        first_weights(SPLIT_AT.index(n))
                    at = lambda place, stage: n == place and stage is not None
                    if b is not None and n < TILES:
                        exps(b, n)
                        if n % 12 == 1 and n > 1:
                            evacuate(b, n // 12 - 1)
                    if at(14, f):
                        second_part(f)
                    if at(17, t):
                        affine2(t)
                    if at(21, f):
                        take_k(f)
                    if at(22, t):
                        gate_exp(t)
                    if at(24, f):
                        take_q(f)
                    if at(25, f):
                        square(f, kx, W.k_clip, W.k_sq)
                    if at(25, f):
                        square2(f, kx, W.k_sq)
                    if at(28, f):
                        square3(f, kx, W.k_sq)
                    if at(28, f):
                        take_v(f)
                    if at(29, f):
                        square(f, qx, W.q_clip, W.q_sq)
                    if at(30, t):
                        take_weights(t)
                    if at(31, f):
                        square2(f, qx, W.q_sq)
                    if at(32, t):
                        act.wait_ge(W.w_kept, t * 16 + 16)
                    if at(34, f):
                        square3(f, qx, W.q_sq)
                    if at(34, g):
                        affine1(g, t)
                    if at(37, g):
                        take_qk(g, 0)
                    if at(39, g):
                        take_qk(g, 1)
                    if at(39, g):
                        take_qk(g, 2)
                    if at(41, g):
                        take_v2(g, b, p)
                    if at(42, g):
                        second_parts(g, 1, qf, qs)
                    if at(43, g):
                        second_parts(g, 2, kf, ks)
                    if at(49, b):
                        evacuate(b, 3)
                    if at(50, f):
                        take_rden(f)
                    if at(53, m):
                        max_parts(m, 0)
                    if at(55, m):
                        max_parts(m, 1)
                    if at(57, b):
                        take_y(b)

            pipelined(act, body)
            act.sem_inc(W.mid_ready, CREDIT)

            def first_part(b, n):
                e, c = n // HC, n % HC
                act.wait_ge(W.mid_ready, b * (E * HC) + n + 1 + CREDIT)
                if c == 0:
                    act.wait_ge(W.y2_mm, b * E + e - 1 + CREDIT)
                a.activation(hidh[e % 2 * HC + c], gel[n % GS], ACT.Copy).then_inc(W.hid_hi, 1)

            def experts(b, p, before, after):
                for n in range(E * HC):
                    act.wait_ge(W.mid_mm, b * (E * HC) + n + 1)
                    act.wait_ge(W.hid_lo, b * (E * HC) + n + 1)
                    a.activation(gel[n % GS], (X, Y)[n % 2][:, :], ACT.Gelu,
                                 bias=col[:, V_EB + n:V_EB + n + 1]).then_inc(W.mid_ready, 1)
                    if n:
                        first_part(b, n - 1)
                    if n == 14 and after:
                        act.wait_ge(W.h2_loaded, b * 16 + 32)
                        a.activation(h2p[0][:, 1 - p, :], h2r[:, 1 - p, :], ACT.Copy).then_inc(W.h2_hi, 1)
                first_part(b, E * HC - 1)

            batches(act, experts)

        @block.gpsimd
        def _(pool):
            g = nc.gpsimd
            g.memset(mhalf[:, :], -0.5).then_inc(W.pool_const, 1)
            pool.wait_ge(W.pool_const, 1)

            def even_orders(f, z, t35, done):
                wait_apart(pool, t35, f * 2 + 1)
                g.tensor_scalar(z[1], z[1], -0.5, None, ALU.add).then_inc(done, 1)
                g.tensor_scalar(z[3], z[3], -0.125, None, ALU.add).then_inc(done, 1)

            def times_q(f):
                pool.wait_ge(W.q_t24, f * 2 + 2)
                pool.wait_ge(W.q_t35, f * 2 + 2)
                for p in range(ORDERS):
                    pool.wait_ge(W.kv_sum, f * ORDERS + p + 1)
                    g.tensor_tensor(kv[:, p, :], qx[p], kv[:, p, :], ALU.mult).then_inc(W.qk_prod, 1)
                for i, (o, a, c) in enumerate([(1, 0, 1), (3, 2, 3), (3, 3, 4), (1, 1, 3)]):
                    if i < 2:
                        pool.wait_ge(W.qk_prod, f * ORDERS + (2, 4)[i])
                    else:
                        pool.wait_ge(W.qk_prod, f * ORDERS + ORDERS)
                        pool.wait_ge(W.n_add, f * 4 + i)
                    g.tensor_tensor(kv[:, o, :], kv[:, a, :], kv[:, c, :], ALU.add).then_inc(W.n_add, 1)

            def body(t, b, m, g_, f, p):
                if g_ is not None:
                    ln_rsqrt("m", g_ * 2)
                if f is not None:
                    ln_rsqrt("a", f)
                if isinstance(f, int) and f == 0:
                    for i in range(2):
                        g.memset(qst[i].rearrange("p h n -> p (h n)").bitcast(F32), 0.0).then_inc(W.stack_set, 1)
                        g.memset(kst[i].rearrange("p h n -> p (h n)").bitcast(F32), TWO_ONES).then_inc(W.stack_set, 1)
                if t is not None:
                    ln_rsqrt("b", t)
                if g_ is not None:
                    ln_rsqrt("m", g_ * 2 + 1)
                if t is not None:
                    xb = xs[:, bass.ds(t * QT, QT), :]
                    wait_apart(pool, W.x2_ready, t + 1)
                    g.tensor_tensor(xb, xb, x2t[:, :, :], ALU.add).then_inc(W.xsum, 1)
                if f is not None:
                    even_orders(f, kx, W.k_t35, W.k_t24)
                    even_orders(f, qx, W.q_t35, W.q_t24)
                if g_ is not None:
                    pool.wait_ge(W.p1_ready, g_ * 2 + 1)
                    g.tensor_tensor(qf[:, :], qf[:, :], qs[:, 0, :], ALU.subtract).then_inc(W.r1_ready, 1)
                    pool.wait_ge(W.p1_ready, g_ * 2 + 2)
                    g.tensor_tensor(kf[:, :], kf[:, :], ks[:, 0, :], ALU.subtract).then_inc(W.r1_ready, 1)
                if f is not None:
                    times_q(f)
                if g_ is not None:
                    if b is not None:
                        wait_apart(pool, W.x2_ready, b + 1)
                    wait_apart(pool, norm["m"]["out"], g_ * 8 + 8)
                    g.tensor_tensor(hk[:, p, :, :], hs[:, :, :], row[:, R_BP:R_BP + D].unsqueeze(1).to_broadcast((P, QT, D)),
                                    ALU.add).then_inc(W.h_kept, 1)

            pipelined(pool, body)

        @block.tensor
        def _(pe):
            k = nc.tensor

            def turn(src, dst, done):
                for t in range(QT):
                    last = k.transpose(dst[:, t * P:(t + 1) * P], src(t), ident)
                last.then_inc(done, 1)

            pe.wait_ge(W.w_loaded, 16 * 12)
            pe.wait_ge(W.w_split, 4)
            pe.wait_ge(W.const_ready, 4)

            def turn_h(f):
                pe.wait_ge(norm["a"]["out"], f * QT + QT)
                if not isinstance(f, int) or f:
                    pe.wait_ge(W.x1_ready, f)
                turn(lambda t: hn[:, t, :], X, W.tr0)

            def project(f, o, dst, done, half):
                terms = TERMS8 if o < 2 else TERMS6
                for i, (wi, hi) in enumerate(terms):
                    if i // (len(terms) // 2) == half:
                        last = k.matmul(dst[:, :], wins[:, wi, o * D:(o + 1) * D], hp[:, hi, :],
                                        start=(i == 0), stop=(i == len(terms) - 1))
                if half:
                    last.then_inc(done, 1)

            def project_k(f, half):
                pe.wait_ge(W.h_split, f + 1)
                project(f, 1, Y, W.hk_mm, half)

            def project_q(f, half):
                project(f, 0, X, W.hq_mm, half)

            def project_v(f, half):
                pe.wait_ge(W.hk_ev, f + 1)
                project(f, 2, Y, W.hv_mm, half)

            def head_sums(f, z, dst, t24, t35, done, evacuated):
                pe.wait_ge(evacuated, f + 1)
                pe.wait_ge(t24, f * 2 + 2)
                pe.wait_ge(t35, f * 2 + 2)
                for p in range(ORDERS):
                    j, var = (p, 0) if p < 4 else (0, 1)
                    last = k.matmul(dst[32 * j:32 * j + 32, :], cst[:, C_SUM + 32 * var:C_SUM + 32 * var + 32], z[p],
                                    start=(p < 4), stop=(p > 0), skip_group_check=True)
                last.then_inc(done, 1)

            def denominators(f):
                pe.wait_ge(W.d_prod, f + 1)
                for t in range(QT):
                    last = k.matmul(X[:, t * H:(t + 1) * H], ksum[:, t * P:(t + 1) * P], cst[:, C_WS:C_WS + H],
                                    start=True, stop=True)
                last.then_inc(W.den_mm, 1)

            def turn_rden(f):
                wait_apart(pe, W.den_rec, f + 1)
                k.transpose(X[0:QT * H, P:2 * P], den[:, :], ident).then_inc(W.rdT_mm, 1)

            def spread_rden(f):
                pe.wait_ge(W.rdT_ev, f + 1)
                for t in range(QT):
                    last = k.matmul(Y[:, t * P:(t + 1) * P], cst[0:QT * H, C_SEL + P * t:C_SEL + P * (t + 1)], rdT[:, :],
                                    start=True, stop=True)
                last.then_inc(W.rdB_mm, 1)

            def output1(f):
                pe.wait_ge(W.outT_ready, f + 1)
                for t in range(QT):
                    last = k.matmul(X[:, t * P:(t + 1) * P], outT[:, t * P:(t + 1) * P], wo_sb[:, :], start=True, stop=True)
                last.then_inc(W.o1_mm, 1)

            def turn_ln(m, f):
                pe.wait_ge(norm["m"]["out"], m * 8 + 8)
                if f is not None:
                    pe.wait_ge(W.hv_ev, f + 1)
                turn(lambda t: ha[:, t, :], Y, W.tr1)

            def project_q2(m, f):
                pe.wait_ge(W.lnT_ready, m + 1)
                if f is not None:
                    pe.wait_ge(W.hq_ev, f + 1)
                k.matmul(X[:, :], wq_sb[:, :], lnT[:, :], start=True, stop=True).then_inc(W.aq_mm, 1)

            def project_k2(m):
                k.matmul(Y[:, :], wk_sb[:, :], lnT[:, :], start=True, stop=True).then_inc(W.ak_mm, 1)

            def project_v2(m):
                pe.wait_ge(W.qf_ready, m + 1)
                for t in range(QT):
                    last = k.matmul(X[:, t * P:(t + 1) * P], lnT[:, t * P:(t + 1) * P], wv_sb[:, :], start=True, stop=True)
                last.then_inc(W.av_mm, 1)

            def maximum(m, n, p):
                head, heads, t = MAXIMA[n]
                if n == 0:
                    pe.wait_ge(W.stack_dma, m * (16 * 12) + 16 * 12)
                if n >= 2:
                    pe.wait_ge(W.smax_red, m * NMAX + n - 1)
                for j in range(heads):
                    h, at = head + j, j * (t + 1) * P
                    k.matmul(ringM[n % 2][:, at:at + (t + 1) * P], qst[p][0:MROW, h, t * P:(t + 1) * P],
                             kst[p][0:MROW, h, 0:(t + 1) * P], start=True, stop=True)
                    last = k.matmul(ringM[n % 2][:, at + t * P:at + (t + 1) * P], identb[:, :], maskA[:, :],
                                    start=False, stop=True, skip_group_check=True)
                last.then_inc(W.smax_mm, 1)

            def turn_maxima(m, b):
                if b is not None:
                    pe.wait_ge(W.pv_ev, b * 4 + 4)
                wait_apart(pe, W.smax_red, m * NMAX + NMAX)
                k.transpose(V[0:QT * H, 0:P], nm[:, :, :].rearrange("p h t -> p (h t)"), ident).then_inc(W.nmT_mm, 1)

            def scores(b, n, p):
                if n == 0:
                    pe.wait_ge(W.max_dma, b * (16 * 3) + 16 * 3)
                else:
                    pe.wait_ge(W.exp_ready, b * TILES + max(n - 1, 1))
                h = 4 * (n // 12) + n % 4
                for t in KEYS[(n // 4) % 3]:
                    at = 2 * P if t == 3 else 0
                    dst = ringE[n % 2]
                    k.matmul(dst[:, at:at + T - t * P], kst[p][0:MROW + 3, h, t * P:(t + 1) * P], qst[p][0:MROW + 3, h, t * P:T],
                             start=True, stop=True)
                    last = k.matmul(dst[:, at:at + P], identb[:, :], maskB[:, :], start=False, stop=True, skip_group_check=True)
                last.then_inc(W.sc_mm, 1)

            def values(b, s_):
                pe.wait_ge(W.exp_ready, b * TILES + 4 * s_ + 4)
                if s_ == 0:
                    pe.wait_ge(W.v_ready, b * QT + QT)
                    if not isinstance(b, int) or b:
                        pe.wait_ge(W.x2_ready, b)
                elif s_ % 3 == 0:
                    pe.wait_ge(W.pv_ev, b * 4 + s_ // 3)
                for t in KEYS[s_ % 3]:
                    at = 2 * P if t == 3 else 0
                    for i in range(4):
                        last = k.matmul(V[32 * i:32 * i + 32, t * P:T], vaug[:, t, 4 * (s_ // 3) + i, :],
                                        pr[:, (4 * s_ + i) % PR, at:at + T - t * P],
                                        start=(t == 0), stop=(t == 3), skip_group_check=True)
                last.then_inc(W.pr_used, 1)

            def turn_back(b, g, t):
                pe.wait_ge(W.pv_ev, b * 4 + g + 1)
                if g == 0 and t is not None:
                    pe.wait_ge(W.lg_ready, t + 1)
                if g == 1 and t is not None:
                    pe.wait_ge(W.xb_ready, t + 1)
                if g:
                    pe.wait_ge(W.y_ready, b * 4 * QT + g * QT)
                turn(lambda t: oT[:, g % 2, t * P:(t + 1) * P], Z, W.ot_tr)

            def turn_y(b):
                pe.wait_ge(W.y_ready, b * 4 * QT + 4 * QT)
                turn(lambda t: yt[:, t, :], Z, W.yT_mm)

            def output2(b, m):
                pe.wait_ge(W.yT_ev, b + 1)
                if m is not None:
                    pe.wait_ge(W.nr_ready, m + 1)
                for t in range(QT):
                    last = k.matmul(V[:, t * P:(t + 1) * P], yT[:, t * P:(t + 1) * P], wp_sb[:, :], start=True, stop=True)
                last.then_inc(W.o2_mm, 1)

            def turn_x2(b):
                pe.wait_ge(norm["b"]["out"], b * QT + QT)
                turn(lambda t: hb[:, t, :], Z, W.tr3)

            def gate(b):
                pe.wait_ge(W.h2_ready, b + 1)
                for t in range(QT):
                    last = k.matmul(Z[:, t * E:(t + 1) * E], h2[:, t * P:(t + 1) * P], gw_sb[:, :], start=True, stop=True)
                last.then_inc(W.gate_mm, 1)

            def turn_weights(t_, b):
                pe.wait_ge(W.wf_ready, t_ + 1)
                if b is not None:
                    pe.wait_ge(W.y_ready, b * 4 * QT + QT)
                for t in range(QT):
                    last = k.transpose(Z[0:E, t * P:(t + 1) * P], wf[:, t, :], ident)
                last.then_inc(W.wfT_mm, 1)

            def bias2(b):
                pe.wait_ge(W.wfT_ev, b + 1)
                for t in range(QT):
                    last = k.matmul(Z[:, t * P:(t + 1) * P], wfT[:, t, :], eb2_sb[:, :], start=True, stop=True)
                last.then_inc(W.b2_mm, 1)

            def body(t, b, m, g, f, p):
                if b is not None:
                    scores(b, 0, p)
                    scores(b, 1, p)
                for n in range(SLOTS):
                    at = lambda place, stage: n == place and stage is not None
                    if m is not None:
                        for i in MAX_AT.get(n, ()):
                            maximum(m, i, 1 - p)
                    if b is not None:
                        if n % 4 == 0 and 0 < n <= TILES:
                            values(b, n // 4 - 1)
                        if n + 2 < TILES:
                            scores(b, n + 2, p)
                    if at(9, f):
                        turn_h(f)
                    if at(13, t):
                        turn_x2(t)
                    if at(17, t):
                        gate(t)
                    if at(17, f):
                        project_k(f, 0)
                    if at(19, f):
                        project_k(f, 1)
                    if at(19, f):
                        project_q(f, 0)
                    if at(20, b):
                        turn_back(b, 0, t)
                    if at(21, f):
                        project_q(f, 1)
                    if at(25, f):
                        project_v(f, 0)
                    if at(25, f):
                        project_v(f, 1)
                    if at(29, t):
                        turn_weights(t, b)
                    if at(31, g):
                        turn_ln(g, f)
                    if at(32, t):
                        bias2(t)
                    if at(35, b):
                        turn_back(b, 1, t)
                    if at(35, g):
                        project_q2(g, f)
                    if at(37, g):
                        project_k2(g)
                    if at(38, g):
                        project_v2(g)
                    if at(39, f):
                        if g is not None:
                            pe.wait_ge(W.kf_ready, g + 1)
                        head_sums(f, qx, Y, W.q_t24, W.q_t35, W.qs_mm, W.hv_ev)
                    if at(41, f):
                        if g is not None:
                            pe.wait_ge(W.v_ev, g + 1)
                        head_sums(f, kx, X, W.k_t24, W.k_t35, W.ks_mm, W.hq_ev)
                    if at(42, b):
                        turn_back(b, 2, t)
                    if at(47, f):
                        denominators(f)
                    if at(50, f):
                        turn_rden(f)
                    if at(50, b):
                        turn_back(b, 3, t)
                    if at(52, f):
                        spread_rden(f)
                    if at(53, m):
                        turn_maxima(m, b)
                    if at(54, b):
                        turn_y(b)
                    if at(56, b):
                        output2(b, m)
                    if at(58, f):
                        output1(f)

            pipelined(pe, body)

            pe.sem_inc(W.y2_mm, CREDIT)

            def hidden(b, p, e, c):
                n = e * HC + c
                if c == 0:
                    pe.wait_ge(W.wl_ready, 2 * e + 1)
                if n == 0:
                    pe.wait_ge(W.h2_lo, b + 1)
                pe.wait_ge(W.mid_ready, b * (E * HC) + n - 1 + CREDIT)
                for i, (wi, hi) in enumerate(TERMS3):
                    last = k.matmul((X, Y)[n % 2][:, :], w1p[wi][:, e, c * P:(c + 1) * P], h2p[hi][:, p, :],
                                    start=(i == 0), stop=(i == len(TERMS3) - 1))
                last.then_inc(W.mid_mm, 1)

            def output(b, e, c):
                if isinstance(b, int) and b == 0 and e == 0 and c == 0:
                    pe.wait_ge(W.xb_ready, B)
                if c == 0:
                    pe.wait_ge(W.wl_ready, 2 * e + 2)
                    pe.wait_ge(W.y_scaled, b * E + e - 1 + CREDIT)
                pe.wait_ge(W.hid_lo, b * (E * HC) + e * HC + c + 1 + GS)
                for i, (hi, wi) in enumerate(TERMS3):
                    last = k.matmul((Z, V)[e % 2][:, :], w2p[wi][:, e * HC + c, :], (hidh, hidl)[hi][e % 2 * HC + c],
                                    start=(c == 0 and i == 0), stop=(c == HC - 1 and i == len(TERMS3) - 1))
                if c == HC - 1:
                    last.then_inc(W.y2_mm, 1)

            def turn_sum(b, p):
                pe.wait_ge(W.acc_ready, b * (E - 1) + E - 1)
                turn(lambda t: acc[p][:, t * P:(t + 1) * P], ringM[p], W.fin_mm)

            def experts(b, p, before, after):
                for c in range(HC):
                    hidden(b, p, 0, c)
                    if before:
                        output(b - 1, E - 1, c)
                for e in range(E - 1):
                    for c in range(HC):
                        hidden(b, p, e + 1, c)
                        output(b, e, c)
                    if e == 0 and before:
                        turn_sum(b - 1, 1 - p)

            batches(pe, experts)
            for c in range(HC):
                output(B - 1, E - 1, c)
            turn_sum(B - 1, 1)


def kernel(**inputs):
    import numpy as _np
    import concourse.bacc as _bacc
    from concourse import mybir as _mybir
    from concourse.bass_utils import run_bass_kernel_spmd as _run

    a = {k: _np.asarray(v) for k, v in inputs.items()}
    f = lambda n: a["L0_ffn_" + n]
    by_width = lambda w: w.reshape(w.shape[:-1] + (H, DH)).swapaxes(-1, -2).reshape(w.shape)
    columns = _np.concatenate([_np.stack([f("ln1_g"), f("ln1_b"), f("ln2_g"), f("ln2_b"), by_width(f("bq")), by_width(f("bk"))], 1),
                               f("exp_b1").reshape(E * HC, P).T], 1)
    rows = _np.tile(_np.concatenate([f("bv"), f("bp"), f("gate_b")])[None], (P, 1))
    arrays = dict(x=a["L0_attn_x"], consts=constants(), cols=columns, rows=rows, w_in=a["L0_attn_W_in"].T,
                  w_out=a["L0_attn_W_out"].T, wq=by_width(f("Wq")), wk=by_width(f("Wk")), wv=f("Wv"), wp=f("Wp"), gate_w=f("gate_W"),
                  ew1=f("exp_W1"), ew2=f("exp_W2"), eb2=f("exp_b2"))
    arrays = {k: _np.ascontiguousarray(v) for k, v in arrays.items()}
    nc = _bacc.Bacc("TRN2", target_bir_lowering=False, num_devices=1)
    args = [nc.dram_tensor(f"in_{k}", v.shape, _mybir.dt.from_np(v.dtype), kind="ExternalInput").ap() for k, v in arrays.items()]
    out = nc.dram_tensor("out_0", (B, T, D), F32, kind="ExternalOutput").ap()
    block_kernel(nc, *args, out)
    r = _run(nc, [{f"in_{k}": v for k, v in arrays.items()}], core_ids=[0])
    return r.results[0]["out_0"]
```
